# Optimizing a Trainium2 kernel written in Bass

```python
import numpy as np
import jax
import jax.numpy as jnp

def _softmax(x, axis=-1):
    return jax.nn.softmax(x, axis=axis)

def _gelu(x):
    return jax.nn.gelu(x, approximate=True)

def _silu(x):
    return jax.nn.silu(x)

def _sigmoid(x):
    return jax.nn.sigmoid(x)

def _layernorm(x, axis=-1, eps=1e-05):
    m = jnp.mean(x, axis=axis, keepdims=True)
    v = jnp.var(x, axis=axis, keepdims=True)
    return (x - m) / jnp.sqrt(v + eps)

def _scatter_add(tgt, idx, src, axis=0):
    return tgt.at[idx].add(src)

def _segment_sum(src, seg, n):
    return jax.ops.segment_sum(src, seg, n)
kernel_name = 'mk_adj_preln_d1_adj_r2_df2ebb'

def setup_inputs(seed: int=0):
    np.random.seed(seed)
    _w = jnp.asarray

    def _rec_inputs():
        import jax
        import jax.numpy as jnp
        _gk = jax.random.key(seed)
        x = -0.0001538 + 1 * jax.random.normal(jax.random.fold_in(_gk, 1), (32, 256, 384), jnp.float32)
        _a = jax.random.bernoulli(jax.random.fold_in(_gk, 2), 0.0625, (32, 256, 256))
        _a = jnp.logical_or(_a, jnp.eye(256, dtype=bool))
        adj = _a
        return (x, adj)
    x, adj = _rec_inputs()

    def _L0_gnn_setup():
        import jax, jax.numpy as jnp
        import numpy as np
        B, S, H = (4, 1024, 384)
        NUM_HEADS = 6
        HEAD_SIZE = H // NUM_HEADS
        NEG = -9000000000000000.0

        def _heads(x):
            b, s, _ = x.shape
            return x.reshape(b, s, NUM_HEADS, HEAD_SIZE).transpose(0, 2, 1, 3)
        key = jax.random.key(seed)
        ks = jax.random.split(key, 10)
        seq_inputs = jax.random.normal(ks[0], (B, S, H), dtype=jnp.float32)
        gm = jax.random.randint(ks[1], (B, S, S), 0, 2) > 0
        graph_mask = gm | jnp.eye(S, dtype=bool)[None]
        sc = 1.0 / np.sqrt(H)
        Wq = jax.random.normal(ks[2], (H, H), dtype=jnp.float32) * sc
        bq = jnp.zeros((H,), dtype=jnp.float32)
        Wk = jax.random.normal(ks[3], (H, H), dtype=jnp.float32) * sc
        bk = jnp.zeros((H,), dtype=jnp.float32)
        Wv = jax.random.normal(ks[4], (H, H), dtype=jnp.float32) * sc
        bv = jnp.zeros((H,), dtype=jnp.float32)
        Wf = jax.random.normal(ks[5], (H, H), dtype=jnp.float32) * sc
        bf = jnp.zeros((H,), dtype=jnp.float32)
        return {'seq_inputs': seq_inputs, 'Wq': Wq, 'bq': bq, 'Wk': Wk, 'bk': bk, 'Wv': Wv, 'bv': bv, 'Wf': Wf, 'bf': bf, 'graph_mask': graph_mask}
    _L0_gnn_all = _L0_gnn_setup()
    _L0_gnn_in = {k: v for k, v in _L0_gnn_all.items() if k in ('Wq', 'bq', 'Wk', 'bk', 'Wv', 'bv', 'Wf', 'bf')}
    del _L0_gnn_all
    return {'x': x, 'adj': adj, 'L0_gnn_Wq': _L0_gnn_in['Wq'], 'L0_gnn_bq': _L0_gnn_in['bq'], 'L0_gnn_Wk': _L0_gnn_in['Wk'], 'L0_gnn_bk': _L0_gnn_in['bk'], 'L0_gnn_Wv': _L0_gnn_in['Wv'], 'L0_gnn_bv': _L0_gnn_in['bv'], 'L0_gnn_Wf': _L0_gnn_in['Wf'], 'L0_gnn_bf': _L0_gnn_in['bf']}

def reference(x, adj, L0_gnn_Wq, L0_gnn_bq, L0_gnn_Wk, L0_gnn_bk, L0_gnn_Wv, L0_gnn_bv, L0_gnn_Wf, L0_gnn_bf):
    import jax
    import jax.numpy as jnp

    def _L0_gnn_ref(seq_inputs, Wq, bq, Wk, bk, Wv, bv, Wf, bf, graph_mask):
        import jax, jax.numpy as jnp
        import numpy as np
        B, S, H = (4, 1024, 384)
        NUM_HEADS = 6
        HEAD_SIZE = H // NUM_HEADS
        NEG = -9000000000000000.0

        def _heads(x):
            b, s, _ = x.shape
            return x.reshape(b, s, NUM_HEADS, HEAD_SIZE).transpose(0, 2, 1, 3)
        q = _heads(seq_inputs @ Wq + bq)
        k = _heads(seq_inputs @ Wk + bk)
        v = _heads(seq_inputs @ Wv + bv)
        scores = jnp.einsum('bhqd,bhkd->bhqk', q, k) / np.sqrt(HEAD_SIZE)
        bias = jnp.where(graph_mask, 0.0, NEG)[:, None]
        probs = jax.nn.softmax(scores + bias, axis=-1)
        ctx = jnp.einsum('bhqk,bhkd->bhqd', probs, v)
        ctx = ctx.transpose(0, 2, 1, 3).reshape(seq_inputs.shape[0], seq_inputs.shape[1], H)
        return ctx @ Wf + bf
    h = jnp.maximum(_layernorm(x, axis=-1), 0.0)
    x = x + _L0_gnn_ref(h, L0_gnn_Wq, L0_gnn_bq, L0_gnn_Wk, L0_gnn_bk, L0_gnn_Wv, L0_gnn_bv, L0_gnn_Wf, L0_gnn_bf, adj)
    return x

_drawn_inputs = setup_inputs


def setup_inputs(seed=0):
    import zlib

    import numpy as np

    out = dict(_drawn_inputs(seed))
    spreads = {'L0_gnn_bq': (0.0, 0.8),
     'L0_gnn_bk': (0.0, 0.8),
     'L0_gnn_bv': (0.0, 0.1),
     'L0_gnn_bf': (0.0, 0.1)}
    factors = {}
    for name, (base, spread) in spreads.items():
        noise = np.random.default_rng([zlib.crc32(name.encode()), seed]).standard_normal(out[name].shape)
        drawn = base * np.exp(spread * noise) if base else spread * noise
        out[name] = jnp.asarray(drawn.astype(out[name].dtype))
    for name, factor in factors.items():
        out[name] = (out[name] * factor).astype(out[name].dtype)
    return out
```

```python
from contextlib import ExitStack

import concourse.bass as bass
from concourse import mybir

F32 = mybir.dt.float32
F16 = mybir.dt.float16
I32 = mybir.dt.int32
ALU = mybir.AluOpType
ACT = mybir.ActivationFunctionType
AX_X = mybir.AxisListType.X
ALL_MAX = bass.bass_isa.ReduceOp.max

P = 128
HEADS = 6
EPS = 1e-5
NEG = -9000000000000000.0
H_SCALE = 2.0 ** 10
P_SCALE = 2.0 ** 14
TOP = 2.0 ** 14
LEAST = 2.0 ** -60
LEAST_QK = 2.0 ** -10
EXPONENT = 0x7F800000
FAR = 3.0e38


def gnn_attention(nc, x, adj, Wq, bq, Wk, bk, Wv, bv, Wf, bf, out):
    B, S, H = x.shape
    D = H // HEADS
    C = H // P
    QT = S // P
    V1 = D + 1
    UNITS = QT * C
    assert D * 2 == P and QT == 2 and C == 3 and B % 2 == 0

    ctx = ExitStack()
    with ctx:
        def sb(name, shape, dt):
            return ctx.enter_context(nc.sbuf_tensor(name, shape, dt))

        def bank(name):
            return ctx.enter_context(nc.psum_tensor(name, [P, 512], F32))

        def sem(name):
            return ctx.enter_context(nc.semaphore(name))

        w_raw = sb("w_raw", [P, 4, C, H], F32)
        w_hi = sb("w_hi", [P, 4, C, H], F16)
        w_lo = sb("w_lo", [P, 4, C, H], F16)
        qk_bias = sb("qk_bias", [P, 2, C], F32)
        qk_bias_s = sb("qk_bias_s", [P, 2, C], F32)
        bv_col = sb("bv_col", [P, C], F32)
        bv_wide = sb("bv_wide", [P, C, P], F32)
        bf_row = sb("bf_row", [1, H], F32)
        ones_row = sb("ones_row", [1, P], F32)
        bf_full = sb("bf_full", [P, H], F32)
        zeros = sb("zeros", [P, P], F32)
        ident = sb("ident", [P, P], F32)
        half = sb("half", [P, QT], F32)
        peak = sb("peak", [P, 6], F32)
        peak_all = sb("peak_all", [P, 6], F32)
        bound = sb("bound", [P, 7], F32)
        scale = sb("scale", [P, 7], F32)
        unscale = sb("unscale", [P, 7], F32)
        w_ratio = sb("w_ratio", [P, 3], F32)
        qk_unscale = sb("qk_unscale", [P, 4], F32)
        qk_scale = sb("qk_scale", [P, 4], F32)
        out_unscale = sb("out_unscale", [P, 1], F32)

        x_in = [sb(f"x_in{p}", [P, QT, H], F32) for p in range(2)]
        adj_in = [sb(f"adj_in{p}", [P, QT, S], adj.dtype) for p in range(2)]
        residual = [sb(f"residual{p}", [P, QT, H], F32) for p in range(2)]
        mask = [sb(f"mask{p}", [P, QT, S], F32) for p in range(2)]
        stats = sb("stats", [P, QT, 6], F32)
        mean_var = sb("mean_var", [P, QT, 2], F32)
        var_s = sb("var_s", [P, QT], F32)
        neg_mean = sb("neg_mean", [P, QT], F32)
        rstd = sb("rstd", [P, QT], F32)
        normed = sb("normed", [P, QT, H], F32)
        h_hi = sb("h_hi", [P, C, S], F16)
        h_lo = sb("h_lo", [P, C, S], F16)
        qk32 = [sb(f"qk32_{j}", [P, 2, S], F32) for j in range(C)]
        split = [sb(f"split{j}", [P, 4, S], F16) for j in range(C)]
        heads = [sb(f"heads{p}", [P, HEADS, 3, S], F16) for p in range(2)]
        v_hi = [sb(f"v_hi{p}", [P, QT, HEADS, V1], F16) for p in range(2)]
        v_lo = [sb(f"v_lo{p}", [P, QT, HEADS, D], F16) for p in range(2)]
        logits = [sb(f"logits{u}", [P, 2, S], F32) for u in range(2)]
        least = [sb(f"least{u}", [P, 2], F32) for u in range(2)]
        probs = [sb(f"probs{u}", [P, 2, S], F32) for u in range(2)]
        pt_hi = [sb(f"pt_hi{u}", [P, 2, QT, P], F16) for u in range(2)]
        pt_lo = [sb(f"pt_lo{u}", [P, 2, QT, P], F16) for u in range(2)]
        inv_sum = [sb(f"inv_sum{t}", [P, HEADS], F32) for t in range(QT)]
        context = [sb(f"context{t}", [P, HEADS, D], F32) for t in range(QT)]
        ct_hi = [sb(f"ct_hi{t}", [P, C, P], F16) for t in range(QT)]
        ct_lo = [sb(f"ct_lo{t}", [P, C, P], F16) for t in range(QT)]
        result = [sb(f"result{t}", [P, H], F32) for t in range(QT)]

        score_bank = [bank("scores0"), bank("scores1")]
        pt_bank = [bank("probs_t0"), bank("probs_t1")]
        ctx_bank = bank("ctx")
        ring = [bank("ring0"), bank("ring1"), bank("ring2")]
        R_HTA, R_HTB, R_OUT0, R_QK0, R_QK1, R_CT1, R_OUT1, R_QK2, R_V0, R_CT0, R_V1 = \
            [ring[n % 3] for n in range(11)]
        R_QK = [R_QK0, R_QK1, R_QK2]
        R_V = [R_V0, R_V1]
        R_CT = [R_CT0, R_CT1]
        R_OUT = [R_OUT0, R_OUT1]
        ctx_ps = ctx_bank[:, 0:HEADS * V1].rearrange("p (h d) -> p h d", h=HEADS)

        w_in = [sem(f"w_in{n}") for n in range(4)]
        small_in = sem("small_in")
        x_loaded = [sem(f"x_loaded{p}") for p in range(2)]
        adj_loaded = [sem(f"adj_loaded{p}") for p in range(2)]
        heads_placed = [sem(f"heads_placed{j}") for j in range(C)]
        out_stored = [sem(f"out_stored{t}") for t in range(QT)]
        dve_chain = sem("dve_chain")
        pool_const = sem("pool_const")
        peak_ready = sem("peak_ready")
        peaks_joined = sem("peaks_joined")
        scales_ready = sem("scales_ready")
        wide_ready = sem("wide_ready")
        w_hi_ready = sem("w_hi_ready")
        w_lo_ready = sem("w_lo_ready")
        bias_ps_ready = sem("bias_ps_ready")
        bf_ready = sem("bf_ready")
        ones_ready = sem("ones_ready")
        passed = sem("passed")
        moments = sem("moments")
        var_ready = sem("var_ready")
        rstd_ready = sem("rstd_ready")
        norm_ready = sem("norm_ready")
        mask_ready = sem("mask_ready")
        residual_ready = sem("residual_ready")
        ht_ready = sem("ht_ready")
        h_hi_ready = sem("h_hi_ready")
        h_lo_ready = sem("h_lo_ready")
        qk_ready = sem("qk_ready")
        qk32_ready = sem("qk32_ready")
        qk_hi_ready = sem("qk_hi_ready")
        qk_lo_ready = sem("qk_lo_ready")
        v_ready = sem("v_ready")
        v_hi_ready = sem("v_hi_ready")
        v_lo_ready = sem("v_lo_ready")
        scores_ready = sem("scores_ready")
        logits_ready = sem("logits_ready")
        probs_ready = sem("probs_ready")
        pt_ready = sem("pt_ready")
        pt_hi_ready = sem("pt_hi_ready")
        pt_lo_ready = sem("pt_lo_ready")
        ctx_ready = sem("ctx_ready")
        inv_ready = sem("inv_ready")
        context_ready = sem("context_ready")
        ct_ready = sem("ct_ready")
        ct_hi_ready = sem("ct_hi_ready")
        ct_lo_ready = sem("ct_lo_ready")
        out_ready = sem("out_ready")
        result_ready = sem("result_ready")

        class Batch:

            def __init__(self, i, k):
                self.i, self.k, self.parity = i, k, k % 2

            def __add__(self, n):
                return Batch(self.i, self.k + n)

            def exists(self):
                return not isinstance(self.i, int) or 0 <= self.k < B

            def index(self):
                return self.i * 2 + self.k

            def count(self, per, extra=0):
                return self.i * (2 * per) + (self.k * per + extra)

            def dma_count(self, per=1):
                return self.i * (16 * per) + (self.k // 2 + 1) * 16 * per

        def wait(eng, s, value):
            if not isinstance(value, int) or value > 0:
                eng.wait_ge(s, value)

        PAIRS_BEFORE_LOOP = 1
        TURNS = (B - 4) // 2
        assert PAIRS_BEFORE_LOOP == 1 and TURNS > 0

        def alone(eng):
            eng.sem_inc(passed, 1)

        def cycles(eng, cycle):
            for k in (-1, 0):
                cycle(Batch(0, k))
            with eng.Fori(0, TURNS) as i:
                cycle(Batch(i, 1))
                cycle(Batch(i, 2))
            for k in range(2 * TURNS + 1, B + 1):
                cycle(Batch(0, k))

        x_v = x.rearrange("b (t p) h -> b p t h", p=P)
        adj_v = adj.rearrange("b (t p) k -> b p t k", p=P)
        out_v = out.rearrange("b (t p) h -> b t p h", p=P)
        block = ctx.enter_context(nc.Block())

        @block.sync
        def _(sp):
            def load_x(b):
                sp.dma_start(x_in[b.parity][:], x_v[b.index()]).then_inc(x_loaded[b.parity], 16)

            def load_adj(b):
                sp.dma_start(adj_in[b.parity][:], adj_v[b.index()]).then_inc(adj_loaded[b.parity], 16)

            def store(b, t):
                wait(sp, result_ready, b.count(2, t + 1))
                sp.dma_start(out_v[b.index(), t], result[t][:]).then_inc(out_stored[t], 16)

            def place_heads(b, j):
                wait(sp, qk_hi_ready, b.count(C, j + 1))
                wait(sp, qk_lo_ready, b.count(C, j + 1))
                for a in range(2):
                    own = slice(D * a, D * a + D)
                    other = slice(D - D * a, 2 * D - D * a)
                    dst, src = heads[b.parity][:, 2 * j + a], split[j]
                    sp.dma_start(dst[own, :, :], src[own, 1:4, :]).then_inc(heads_placed[j], 16)
                    sp.dma_start(dst[other, 0, :], src[own, 0, :]).then_inc(heads_placed[j], 16)
                    sp.dma_start(dst[other, 1:3, :], src[own, 2:4, :]).then_inc(heads_placed[j], 16)

            load_x(Batch(0, 0))
            for n, W in enumerate((Wq, Wk, Wv, Wf)):
                sp.dma_start(w_raw[:, n], W.rearrange("(c p) n -> p c n", p=P)).then_inc(w_in[n], 16)
            sp.dma_start(qk_bias[:, 0], bq.rearrange("(c p) -> p c", p=P),
                         allow_slow_non_contiguous=True).then_inc(small_in, 16)
            sp.dma_start(qk_bias[:, 1], bk.rearrange("(c p) -> p c", p=P),
                         allow_slow_non_contiguous=True).then_inc(small_in, 16)
            sp.dma_start(bv_col[:], bv.rearrange("(c p) -> p c", p=P),
                         allow_slow_non_contiguous=True).then_inc(small_in, 16)
            sp.dma_start(bf_row[:], bf.rearrange("(a n) -> a n", a=1)).then_inc(small_in, 16)
            load_adj(Batch(0, 0))
            load_x(Batch(0, 1))
            load_adj(Batch(0, 1))

            def cycle(b):
                if (b + -1).exists():
                    store(b + -1, 0)
                if (b + 3).exists() and (b + 1).exists():
                    wait(sp, mask_ready, (b + 1).count(2, 2))
                    load_adj(b + 3)
                if (b + 1).exists():
                    place_heads(b + 1, 0)
                    place_heads(b + 1, 1)
                if (b + -1).exists():
                    store(b + -1, 1)
                if (b + 3).exists() and (b + 1).exists():
                    wait(sp, residual_ready, (b + 1).count(2, 2))
                    load_x(b + 3)
                if (b + 1).exists():
                    place_heads(b + 1, 2)

            cycles(sp, cycle)
            for t in range(QT):
                sp.wait_ge(out_stored[t], 16 * B)

        @block.gpsimd
        def _(pool):
            def normalise(b):
                wait(pool, var_ready, b.count(2, 2))
                pool.tensor_tensor(rstd[:], var_s[:], half[:], ALU.pow).then_inc(rstd_ready, 1)
                pool.wait_ge(rstd_ready, b.count(1, 1))
                wait(pool, ht_ready, b.count(2, 0))
                alone(pool)
                for t in range(QT):
                    pool.tensor_scalar(normed[:, t], x_in[b.parity][:, t], neg_mean[:, t:t + 1],
                                       rstd[:, t:t + 1], ALU.add, ALU.mult).then_inc(norm_ready, 1)

            def make_mask(b):
                wait(pool, adj_loaded[b.parity], b.dma_count())
                wait(pool, logits_ready, (b + -1).count(2 * UNITS, 0))
                alone(pool)
                for t in range(QT):
                    pool.tensor_scalar(mask[b.parity][:, t], adj_in[b.parity][:, t], -1.0,
                                       qk_scale[:, 1:2], ALU.add, ALU.mult).then_inc(mask_ready, 1)

            def split_lo(b, j):
                wait(pool, qk_hi_ready, b.count(C, j + 1))
                pool.tensor_tensor(split[j][:, 0:4:3, :], qk32[j][:], split[j][:, 1:3, :],
                                   ALU.subtract).then_inc(qk_lo_ready, 1)

            def add_bias(b):
                wait(pool, x_loaded[b.parity], b.dma_count())
                wait(pool, result_ready, (b + -1).count(2, 0))
                for t in range(QT):
                    pool.tensor_tensor(residual[b.parity][:, t], x_in[b.parity][:, t], bf_full[:],
                                       ALU.add).then_inc(residual_ready, 1)

            pool.memset(ident[:], 0.0).then_inc(pool_const, 1)
            pool.memset(half[:], -0.5).then_inc(pool_const, 1)
            pool.memset(ones_row[:], 1.0).then_inc(pool_const, 1)
            pool.wait_ge(pool_const, 3)
            pool.affine_select(out=ident[:], in_=ident[:], compare_op=ALU.not_equal, fill=1.0, base=0,
                               pattern=[[-1, P]], channel_multiplier=1).then_inc(pool_const, 1)
            pool.wait_ge(peak_ready, 6)
            pool.partition_all_reduce(peak_all[:], peak[:], P, ALL_MAX).then_inc(peaks_joined, 1)
            wait(pool, x_loaded[0], 16)
            normalise(Batch(0, 0))
            pool.wait_ge(scales_ready, 1)
            pool.wait_ge(bf_ready, 1)

            def cycle(b):
                if (b + 1).exists():
                    make_mask(b + 1)
                    split_lo(b + 1, 0)
                    split_lo(b + 1, 1)
                    add_bias(b + 1)
                if (b + 2).exists():
                    normalise(b + 2)
                if (b + 1).exists():
                    split_lo(b + 1, 2)

            cycles(pool, cycle)

        @block.scalar
        def _(act):
            def exps(b, u):
                for a in range(2):
                    wait(act, logits_ready, b.count(2 * UNITS, 2 * u + a + 1))
                    act.activation(probs[u % 2][:, a], logits[u % 2][:, a], ACT.Exp,
                                   bias=least[u % 2][:, a:a + 1], scale=-1.0).then_inc(probs_ready, 1)

            def probs_hi(b, u):
                wait(act, pt_ready, b.count(UNITS, u + 1))
                act.activation(pt_hi[u % 2][:].rearrange("p a t q -> p (a t q)"), pt_bank[u % 2][:],
                               ACT.Copy, scale=P_SCALE).then_inc(pt_hi_ready, 1)

            def h_hi_part(b):
                for n, (c0, c1, src) in enumerate(((0, 2, R_HTA), (2, 3, R_HTB))):
                    wait(act, ht_ready, b.count(2, n + 1))
                    act.activation(h_hi[:, c0:c1].rearrange("p c s -> p (c s)"),
                                   src[:, 0:(c1 - c0) * S], ACT.Relu).then_inc(h_hi_ready, 1)

            def qk_full(b, j):
                wait(act, qk_ready, b.count(C, j + 1))
                for n in range(2):
                    act.activation(qk32[j][:, n], R_QK[j][:, n * S:(n + 1) * S], ACT.Identity,
                                   bias=qk_bias_s[:, n, j:j + 1], scale=w_ratio[:, n:n + 1])\
                       .then_inc(qk32_ready, 1)

            def v_hi_part(b, t):
                wait(act, v_ready, b.count(2, t + 1))
                act.activation(v_hi[b.parity][:, t, :, 0:D], R_V[t][:, 0:H].rearrange("p (h d) -> p h d", d=D),
                               ACT.Copy, scale=w_ratio[:, 2:3]).then_inc(v_hi_ready, 1)

            def context_hi(b, t):
                wait(act, ct_ready, b.count(2, t + 1))
                act.activation(ct_hi[t][:].rearrange("p c q -> p (c q)"), R_CT[t][:, 0:H],
                               ACT.Copy).then_inc(ct_hi_ready, 1)

            act.wait_ge(scales_ready, 1)
            for n in range(4):
                act.activation(w_hi[:, n].rearrange("p c n -> p (c n)"), w_raw[:, n].rearrange("p c n -> p (c n)"),
                               ACT.Copy, scale=scale[:, n:n + 1]).then_inc(w_hi_ready, 1)

            def cycle(b):
                here, before, front = b.exists(), (b + -1).exists(), (b + 1).exists()

                def hi_of(u):
                    if u == 0:
                        if before:
                            probs_hi(b + -1, UNITS - 1)
                    elif here:
                        probs_hi(b, u - 1)

                if here:
                    exps(b, 0)
                if front:
                    h_hi_part(b + 1)
                hi_of(0)
                if here:
                    exps(b, 1)
                if front:
                    qk_full(b + 1, 0)
                hi_of(1)
                if here:
                    exps(b, 2)
                if front:
                    qk_full(b + 1, 1)
                hi_of(2)
                if before:
                    context_hi(b + -1, 1)
                if here:
                    exps(b, 3)
                hi_of(3)
                if here:
                    exps(b, 4)
                if front:
                    qk_full(b + 1, 2)
                hi_of(4)
                if here:
                    exps(b, 5)
                if front:
                    v_hi_part(b + 1, 0)
                hi_of(5)
                if here:
                    context_hi(b, 0)
                if front:
                    v_hi_part(b + 1, 1)

            cycles(act, cycle)

        @block.vector
        def _(dve):
            chain = [0]

            def step(instruction):
                chain[0] += 1
                instruction.then_inc(dve_chain, 1)
                dve.wait_ge(dve_chain, chain[0])

            def mask_and_max(b, u):
                t, j = u // C, u % C
                wait(dve, scores_ready, b.count(UNITS, u + 1))
                if u == 0:
                    wait(dve, mask_ready, b.count(2, 2))
                alone(dve)
                for a in range(2):
                    dve.tensor_tensor_reduce(
                        out=logits[u % 2][:, a], in0=score_bank[u % 2][:, a * S:(a + 1) * S],
                        in1=mask[b.parity][:, t], scale=qk_unscale[:, 2:3], scalar=FAR,
                        op0=ALU.add, op1=ALU.min, accum_out=least[u % 2][:, a:a + 1]).then_inc(logits_ready, 1)

            def probs_lo(b, u):
                wait(dve, pt_hi_ready, b.count(UNITS, u + 1))
                dve.scalar_tensor_tensor(
                    out=pt_lo[u % 2][:].rearrange("p a t q -> p (a t q)"), in0=pt_bank[u % 2][:],
                    scalar=P_SCALE, in1=pt_hi[u % 2][:].rearrange("p a t q -> p (a t q)"),
                    op0=ALU.mult, op1=ALU.subtract).then_inc(pt_lo_ready, 1)

            def h_lo_part(b):
                for n, (c0, c1, src) in enumerate(((0, 2, R_HTA), (2, 3, R_HTB))):
                    wait(dve, h_hi_ready, b.count(2, n + 1))
                    dve.scalar_tensor_tensor(
                        out=h_lo[:, c0:c1].rearrange("p c s -> p (c s)"), in0=src[:, 0:(c1 - c0) * S],
                        scalar=0.0, in1=h_hi[:, c0:c1].rearrange("p c s -> p (c s)"),
                        op0=ALU.max, op1=ALU.subtract).then_inc(h_lo_ready, 1)

            def qk_hi_part(b, j):
                wait(dve, qk32_ready, b.count(2 * C, 2 * j + 2))
                dve.tensor_copy(split[j][:, 1:3], qk32[j][:]).then_inc(qk_hi_ready, 1)

            def v_lo_part(b, t):
                wait(dve, v_hi_ready, b.count(2, t + 1))
                dve.scalar_tensor_tensor(
                    out=v_lo[b.parity][:, t], in0=R_V[t][:, 0:H].rearrange("p (h d) -> p h d", d=D),
                    scalar=w_ratio[:, 2:3], in1=v_hi[b.parity][:, t, :, 0:D],
                    op0=ALU.mult, op1=ALU.subtract).then_inc(v_lo_ready, 1)

            def divide(b, t):
                wait(dve, ctx_ready, b.count(UNITS, C * (t + 1)))
                dve.reciprocal(inv_sum[t][:], ctx_ps[:, :, D]).then_inc(inv_ready, 1)
                dve.wait_ge(inv_ready, b.count(2, t + 1))
                dve.tensor_tensor(context[t][:], ctx_ps[:, :, 0:D],
                                  inv_sum[t][:].unsqueeze(2).to_broadcast([P, HEADS, D]),
                                  ALU.mult).then_inc(context_ready, 1)

            def context_lo(b, t):
                wait(dve, ct_hi_ready, b.count(2, t + 1))
                dve.tensor_tensor(ct_lo[t][:].rearrange("p c q -> p (c q)"), R_CT[t][:, 0:H],
                                  ct_hi[t][:].rearrange("p c q -> p (c q)"),
                                  ALU.subtract).then_inc(ct_lo_ready, 1)

            def finish(b, t):
                wait(dve, out_ready, b.count(2, t + 1))
                wait(dve, residual_ready, b.count(2, t + 1))
                wait(dve, out_stored[t], b.count(16, 0))
                dve.scalar_tensor_tensor(out=result[t][:], in0=R_OUT[t][:, 0:H], scalar=out_unscale[:, 0:1],
                                         in1=residual[b.parity][:, t], op0=ALU.mult,
                                         op1=ALU.add).then_inc(result_ready, 1)

            def layer_stats(b):
                wait(dve, x_loaded[b.parity], b.dma_count())
                for t in range(QT):
                    dve.bn_stats(out=stats[:, t], in_=x_in[b.parity][:, t]).then_inc(moments, 1)
                for t in range(QT):
                    dve.wait_ge(moments, b.count(4, t + 1))
                    alone(dve)
                    dve.bn_aggr(out=mean_var[:, t], in_=stats[:, t]).then_inc(moments, 1)
                dve.wait_ge(moments, b.count(4, 4))
                wait(dve, norm_ready, b.count(2, 0))
                dve.tensor_scalar(var_s[:], mean_var[:, :, 1], EPS, H_SCALE ** -2, ALU.add,
                                  ALU.mult).then_inc(var_ready, 1)
                dve.tensor_scalar(neg_mean[:], mean_var[:, :, 0], -1.0, None,
                                  ALU.mult).then_inc(var_ready, 1)

            step(dve.memset(zeros[:], 0.0))
            for p in range(2):
                dve.memset(v_hi[p][:, :, :, D:V1], 1.0).then_inc(ones_ready, 1)
            dve.wait_ge(small_in, 64)
            for n in range(2):
                dve.tensor_reduce(peak[:, 4 + n:5 + n], qk_bias[:, n], AX_X, ALU.max,
                                  apply_absolute_value=True).then_inc(peak_ready, 1)
            for c in range(C):
                dve.tensor_scalar(bv_wide[:, c], zeros[:], bv_col[:, c:c + 1], None,
                                  ALU.add).then_inc(wide_ready, 1)
            layer_stats(Batch(0, 0))
            for n in range(4):
                dve.wait_ge(w_in[n], 16)
                dve.tensor_reduce(peak[:, n:n + 1], w_raw[:, n].rearrange("p c n -> p (c n)"), AX_X, ALU.max,
                                  apply_absolute_value=True).then_inc(peak_ready, 1)
            dve.wait_ge(peaks_joined, 1)
            step(dve.tensor_copy(bound[:, 0:4], peak_all[:, 0:4]))
            step(dve.scalar_tensor_tensor(out=bound[:, 4:6], in0=peak_all[:, 0:2], scalar=float(H),
                                          in1=peak_all[:, 4:6], op0=ALU.mult, op1=ALU.add))
            step(dve.tensor_scalar(bound[:, 6:7], peak_all[:, 2:3], float(H), None, ALU.mult))
            step(dve.tensor_scalar(bound[:], bound[:], LEAST, None, ALU.max))
            step(dve.tensor_scalar(bound[:, 4:6], bound[:, 4:6], LEAST_QK, None, ALU.max))
            step(dve.tensor_scalar(bound[:].bitcast(I32), bound[:].bitcast(I32), EXPONENT, None,
                                   ALU.bitwise_and))
            step(dve.tensor_scalar(unscale[:], bound[:], 1.0 / TOP, None, ALU.mult))
            step(dve.reciprocal(scale[:], unscale[:]))
            step(dve.tensor_tensor(w_ratio[:], scale[:, 4:7], unscale[:, 0:3], ALU.mult))
            step(dve.tensor_scalar(w_ratio[:], w_ratio[:], 1.0 / H_SCALE, None, ALU.mult))
            step(dve.tensor_tensor(qk_unscale[:, 0:1], unscale[:, 4:5], unscale[:, 5:6], ALU.mult))
            step(dve.tensor_scalar(qk_unscale[:, 2:3], qk_unscale[:, 0:1], -1.0 / D ** 0.5, None, ALU.mult))
            step(dve.tensor_tensor(qk_scale[:, 0:1], scale[:, 4:5], scale[:, 5:6], ALU.mult))
            step(dve.tensor_scalar(qk_scale[:, 1:2], qk_scale[:, 0:1], -NEG * D ** 0.5, None, ALU.mult))
            step(dve.tensor_tensor(out_unscale[:], unscale[:, 6:7], unscale[:, 3:4], ALU.mult))
            for n in range(2):
                step(dve.tensor_scalar(qk_bias_s[:, n], qk_bias[:, n], scale[:, 4 + n:5 + n], None, ALU.mult))
            step(dve.memset(zeros[:], 0.0))
            dve.memset(zeros[:, 0:1], 0.0).then_inc(scales_ready, 1)
            dve.wait_ge(bias_ps_ready, 1)
            dve.tensor_copy(bf_full[:], ctx_bank[:, 0:H]).then_inc(bf_ready, 1)
            for n in range(4):
                dve.wait_ge(w_hi_ready, n + 1)
                dve.scalar_tensor_tensor(
                    out=w_lo[:, n].rearrange("p c n -> p (c n)"), in0=w_raw[:, n].rearrange("p c n -> p (c n)"),
                    scalar=scale[:, n:n + 1], in1=w_hi[:, n].rearrange("p c n -> p (c n)"),
                    op0=ALU.mult, op1=ALU.subtract).then_inc(w_lo_ready, 1)

            def cycle(b):
                here, before, front = b.exists(), (b + -1).exists(), (b + 1).exists()

                def lo_of(u):
                    if u == 0:
                        if before:
                            probs_lo(b + -1, UNITS - 1)
                    elif here:
                        probs_lo(b, u - 1)

                if here:
                    mask_and_max(b, 0)
                if front:
                    h_lo_part(b + 1)
                lo_of(0)
                if before:
                    finish(b + -1, 0)
                if here:
                    mask_and_max(b, 1)
                if front:
                    qk_hi_part(b + 1, 0)
                lo_of(1)
                if before:
                    divide(b + -1, 1)
                if here:
                    mask_and_max(b, 2)
                if front:
                    qk_hi_part(b + 1, 1)
                lo_of(2)
                if before:
                    context_lo(b + -1, 1)
                if here:
                    mask_and_max(b, 3)
                if before:
                    finish(b + -1, 1)
                if (b + 2).exists():
                    layer_stats(b + 2)
                lo_of(3)
                if here:
                    mask_and_max(b, 4)
                if front:
                    qk_hi_part(b + 1, 2)
                lo_of(4)
                if here:
                    divide(b, 0)
                if here:
                    mask_and_max(b, 5)
                if front:
                    v_lo_part(b + 1, 0)
                lo_of(5)
                if here:
                    context_lo(b, 0)
                if front:
                    v_lo_part(b + 1, 1)

            cycles(dve, cycle)

        @block.tensor
        def _(pe):
            def three(out_ap, a_hi, a_lo, m_hi, m_lo, first, last):
                pe.matmul(out_ap, a_hi, m_hi, start=first, stop=False)
                pe.matmul(out_ap, a_hi, m_lo, start=False, stop=False)
                return pe.matmul(out_ap, a_lo, m_hi, start=False, stop=last)

            def transpose_h(b):
                for t in range(QT):
                    wait(pe, norm_ready, b.count(2, t + 1))
                for n, (c0, c1, dst) in enumerate(((0, 2, R_HTA), (2, 3, R_HTB))):
                    if n == 0 and (b + -2).exists():
                        wait(pe, ct_lo_ready, (b + -2).count(2, 1))
                    if n == 1:
                        wait(pe, v_lo_ready, b.count(2, 0))
                    for c in range(c0, c1):
                        for t in range(QT):
                            o = (c - c0) * S + t * P
                            mm = pe.transpose(dst[:, o:o + P], normed[:, t, c * P:(c + 1) * P], ident[:])
                    mm.then_inc(ht_ready, 1)

            def project_qk(b, j):
                if j == 0:
                    wait(pe, h_lo_ready, b.count(2, 2))
                if j == 2:
                    wait(pe, qk32_ready, b.count(2 * C, 4))
                for n in range(2):
                    for c in range(C):
                        col = slice(j * P, (j + 1) * P)
                        mm = three(R_QK[j][:, n * S:(n + 1) * S], w_hi[:, n, c, col], w_lo[:, n, c, col],
                                   h_hi[:, c], h_lo[:, c], c == 0, c == C - 1)
                mm.then_inc(qk_ready, 1)

            def project_v(b, t):
                if t == 0:
                    if (b + -2).exists():
                        wait(pe, ct_lo_ready, (b + -2).count(2, 2))
                else:
                    wait(pe, qk32_ready, b.count(2 * C, 6))
                for c in range(C):
                    tok = slice(t * P, (t + 1) * P)
                    mm = three(R_V[t][:, 0:H], h_hi[:, c, tok], h_lo[:, c, tok],
                               w_hi[:, 2, c], w_lo[:, 2, c], c == 0, c == C - 1)
                mm.then_inc(v_ready, 1)

            def scores(b, u):
                t, j = u // C, u % C
                if t == 0:
                    wait(pe, heads_placed[j], b.count(6 * 16, 6 * 16))
                wait(pe, logits_ready, b.count(2 * UNITS, 2 * u - 2))
                for a in range(2):
                    h = heads[b.parity][:, 2 * j + a]
                    q = h[:, 0, t * P:(t + 1) * P]
                    o = score_bank[u % 2][:, a * S:(a + 1) * S]
                    pe.matmul(o, q, h[:, 1], start=True, stop=False)
                    mm = pe.matmul(o, q, h[:, 2], start=False, stop=True)
                mm.then_inc(scores_ready, 1)

            def transpose_probs(b, u):
                wait(pe, pt_lo_ready, b.count(UNITS, u - 1))
                for a in range(2):
                    wait(pe, probs_ready, b.count(2 * UNITS, 2 * u + a + 1))
                    for s in range(QT):
                        o = (a * QT + s) * P
                        mm = pe.transpose(pt_bank[u % 2][:, o:o + P], probs[u % 2][:, a, s * P:(s + 1) * P],
                                          ident[:])
                mm.then_inc(pt_ready, 1)

            def apply_probs(b, u):
                t, j = u // C, u % C
                wait(pe, pt_lo_ready, b.count(UNITS, u + 1))
                if u == 0:
                    wait(pe, v_lo_ready, b.count(2, 2))
                if j == 0:
                    wait(pe, context_ready, b.count(2, t))
                for a in range(2):
                    h = 2 * j + a
                    for s in range(QT):
                        hi, lo = pt_hi[u % 2][:, a, s], pt_lo[u % 2][:, a, s]
                        vh, vl = v_hi[b.parity][:, s, h], v_lo[b.parity][:, s, h]
                        pe.matmul(ctx_ps[:, h], hi, vh, start=(s == 0), stop=False)
                        pe.matmul(ctx_ps[:, h, 0:D], hi, vl, start=False, stop=False)
                        mm = pe.matmul(ctx_ps[:, h], lo, vh, start=False, stop=(s == QT - 1))
                mm.then_inc(ctx_ready, 1)

            def transpose_context(b, t):
                wait(pe, context_ready, b.count(2, t + 1))
                if t == 1:
                    wait(pe, result_ready, b.count(2, 1))
                else:
                    wait(pe, result_ready, b.count(2, 0))
                for c in range(C):
                    mm = pe.transpose(R_CT[t][:, c * P:(c + 1) * P],
                                      context[t][:, 2 * c:2 * c + 2].rearrange("p h d -> p (h d)"), ident[:])
                mm.then_inc(ct_ready, 1)

            def project_out(b, t):
                wait(pe, ct_lo_ready, b.count(2, t + 1))
                if t == 0:
                    if (b + 1).exists():
                        wait(pe, v_lo_ready, (b + 1).count(2, 1))
                elif (b + 2).exists():
                    wait(pe, qk32_ready, (b + 2).count(2 * C, 2))
                for c in range(C):
                    mm = three(R_OUT[t][:, 0:H], ct_hi[t][:, c], ct_lo[t][:, c],
                               w_hi[:, 3, c], w_lo[:, 3, c], c == 0, c == C - 1)
                mm.then_inc(out_ready, 1)

            pe.wait_ge(pool_const, 4)
            pe.wait_ge(small_in, 64)
            pe.wait_ge(wide_ready, C)
            pe.wait_ge(w_in[3], 16)
            pe.matmul(ctx_bank[:, 0:H], ones_row[:], bf_row[:], start=True, stop=False)
            for c in range(C):
                mm = pe.matmul(ctx_bank[:, 0:H], bv_wide[:, c], w_raw[:, 3, c], start=False, stop=(c == C - 1))
            mm.then_inc(bias_ps_ready, 1)
            pe.wait_ge(bf_ready, 1)
            pe.wait_ge(ones_ready, 2)

            def cycle(b):
                here, before, front = b.exists(), (b + -1).exists(), (b + 1).exists()

                def transpose_of(u):
                    if u == 0:
                        if before:
                            transpose_probs(b + -1, UNITS - 1)
                    elif here:
                        transpose_probs(b, u - 1)

                def apply_of(u):
                    if u < 2:
                        if before:
                            apply_probs(b + -1, UNITS - 2 + u)
                    elif here:
                        apply_probs(b, u - 2)

                if here:
                    scores(b, 0)
                if front:
                    transpose_h(b + 1)
                transpose_of(0)
                if before:
                    project_out(b + -1, 0)
                apply_of(0)
                if here:
                    scores(b, 1)
                if front:
                    if b.k == -1:
                        pe.wait_ge(w_lo_ready, 4)
                    project_qk(b + 1, 0)
                transpose_of(1)
                apply_of(1)
                if here:
                    scores(b, 2)
                if front:
                    project_qk(b + 1, 1)
                transpose_of(2)
                if before:
                    transpose_context(b + -1, 1)
                apply_of(2)
                if here:
                    scores(b, 3)
                if before:
                    project_out(b + -1, 1)
                transpose_of(3)
                apply_of(3)
                if here:
                    scores(b, 4)
                if front:
                    project_qk(b + 1, 2)
                transpose_of(4)
                apply_of(4)
                if here:
                    scores(b, 5)
                if front:
                    project_v(b + 1, 0)
                transpose_of(5)
                if here:
                    transpose_context(b, 0)
                apply_of(5)
                if front:
                    project_v(b + 1, 1)

            cycles(pe, cycle)


_INS = ['x', 'adj', 'L0_gnn_Wq', 'L0_gnn_bq', 'L0_gnn_Wk', 'L0_gnn_bk', 'L0_gnn_Wv', 'L0_gnn_bv',
        'L0_gnn_Wf', 'L0_gnn_bf']


def kernel(**inputs):
    import numpy as _np
    import concourse.bacc as _bacc
    from concourse import mybir as _mybir
    from concourse.bass_utils import run_bass_kernel_spmd as _run

    nc = _bacc.Bacc("TRN2", target_bir_lowering=False, num_devices=1)
    arrays, args = {}, []
    for name in _INS:
        a = _np.ascontiguousarray(inputs[name])
        arrays[f"in_{name}_dram"] = a
        args.append(nc.dram_tensor(f"in_{name}_dram", a.shape, _mybir.dt.from_np(a.dtype), kind="ExternalInput").ap())
    args.append(nc.dram_tensor("out_0_dram", inputs['x'].shape, F32, kind="ExternalOutput").ap())
    gnn_attention(nc, *args)
    r = _run(nc, [arrays], core_ids=[0])
    return r.results[0]["out_0_dram"]
```

```python
from contextlib import ExitStack

import concourse.bass as bass
from concourse import mybir

F32 = mybir.dt.float32
F16 = mybir.dt.float16
I32 = mybir.dt.int32
ALU = mybir.AluOpType
ACT = mybir.ActivationFunctionType
AX_X = mybir.AxisListType.X
ALL_MAX = bass.bass_isa.ReduceOp.max

P = 128
HEADS = 6
EPS = 1e-5
NEG = -9000000000000000.0
H_SCALE = 2.0 ** 10
P_SCALE = 2.0 ** 14
TOP = 2.0 ** 14
LEAST = 2.0 ** -60
LEAST_QK = 2.0 ** -10
EXPONENT = 0x7F800000
FAR = 3.0e38


def gnn_attention(nc, x, adj, Wq, bq, Wk, bk, Wv, bv, Wf, bf, out):
    B, S, H = x.shape
    D = H // HEADS
    C = H // P
    QT = S // P
    V1 = D + 1
    UNITS = QT * C
    assert D * 2 == P and QT == 2 and C == 3 and B % 2 == 0

    ctx = ExitStack()
    with ctx:
        def sb(name, shape, dt):
            return ctx.enter_context(nc.sbuf_tensor(name, shape, dt))

        def bank(name):
            return ctx.enter_context(nc.psum_tensor(name, [P, 512], F32))

        def sem(name):
            return ctx.enter_context(nc.semaphore(name))

        w_raw = sb("w_raw", [P, 4, C, H], F32)
        w_hi = sb("w_hi", [P, 4, C, H], F16)
        w_lo = sb("w_lo", [P, 4, C, H], F16)
        qk_bias = sb("qk_bias", [P, 2, C], F32)
        qk_bias_s = sb("qk_bias_s", [P, 2, C], F32)
        bv_col = sb("bv_col", [P, C], F32)
        bv_wide = sb("bv_wide", [P, C, P], F32)
        bf_row = sb("bf_row", [1, H], F32)
        ones_row = sb("ones_row", [1, P], F32)
        bf_full = sb("bf_full", [P, H], F32)
        zeros = sb("zeros", [P, P], F32)
        ident = sb("ident", [P, P], F32)
        half = sb("half", [P, QT], F32)
        qk_peak = sb("qk_peak", [P, 4], F32)
        qk_peak_all = sb("qk_peak_all", [P, 4], F32)
        qk_bound = sb("qk_bound", [P, 4], F32)
        qk_scale = sb("qk_scale", [P, 4], F32)
        qk_unscale = sb("qk_unscale", [P, 4], F32)
        vf_peak = sb("vf_peak", [P, 2], F32)
        vf_peak_all = sb("vf_peak_all", [P, 2], F32)
        vf_bound = sb("vf_bound", [P, 3], F32)
        vf_scale = sb("vf_scale", [P, 3], F32)
        vf_unscale = sb("vf_unscale", [P, 3], F32)
        qk_ratio = sb("qk_ratio", [P, 2], F32)
        v_ratio = sb("v_ratio", [P, 1], F32)
        logit_product = sb("logit_product", [P, 2], F32)
        logit_unscale = sb("logit_unscale", [P, 1], F32)
        mask_scale = sb("mask_scale", [P, 1], F32)
        out_unscale = sb("out_unscale", [P, 1], F32)

        x_in = [sb(f"x_in{p}", [P, QT, H], F32) for p in range(2)]
        adj_in = [sb(f"adj_in{p}", [P, QT, S], adj.dtype) for p in range(2)]
        residual = [sb(f"residual{p}", [P, QT, H], F32) for p in range(2)]
        mask = [sb(f"mask{p}", [P, QT, S], F32) for p in range(2)]
        stats = sb("stats", [P, QT, 6], F32)
        mean_var = sb("mean_var", [P, QT, 2], F32)
        var_s = sb("var_s", [P, QT], F32)
        neg_mean = sb("neg_mean", [P, QT], F32)
        rstd = sb("rstd", [P, QT], F32)
        normed = sb("normed", [P, QT, H], F32)
        h_hi = sb("h_hi", [P, C, S], F16)
        h_lo = sb("h_lo", [P, C, S], F16)
        qk32 = [sb(f"qk32_{j}", [P, 2, S], F32) for j in range(C)]
        split = [sb(f"split{j}", [P, 4, S], F16) for j in range(C)]
        heads = [sb(f"heads{p}", [P, HEADS, 3, S], F16) for p in range(2)]
        v_hi = [sb(f"v_hi{p}", [P, QT, HEADS, V1], F16) for p in range(2)]
        v_lo = [sb(f"v_lo{p}", [P, QT, HEADS, D], F16) for p in range(2)]
        logits = [sb(f"logits{u}", [P, 2, S], F32) for u in range(2)]
        least = [sb(f"least{u}", [P, 2], F32) for u in range(2)]
        probs = [sb(f"probs{u}", [P, 2, S], F32) for u in range(2)]
        pt_hi = [sb(f"pt_hi{u}", [P, 2, QT, P], F16) for u in range(2)]
        pt_lo = [sb(f"pt_lo{u}", [P, 2, QT, P], F16) for u in range(2)]
        inv_sum = [sb(f"inv_sum{t}", [P, HEADS], F32) for t in range(QT)]
        context = [sb(f"context{t}", [P, HEADS, D], F32) for t in range(QT)]
        ct_hi = [sb(f"ct_hi{t}", [P, C, P], F16) for t in range(QT)]
        ct_lo = [sb(f"ct_lo{t}", [P, C, P], F16) for t in range(QT)]
        result = [sb(f"result{t}", [P, H], F32) for t in range(QT)]

        score_bank = [bank("scores0"), bank("scores1")]
        pt_bank = [bank("probs_t0"), bank("probs_t1")]
        ctx_bank = bank("ctx")
        ring = [bank("ring0"), bank("ring1"), bank("ring2")]
        R_HT = ring[0:2]
        R_QK = [ring[0], ring[1], ring[1]]
        R_V = ring[0:2]
        R_CT = [ring[2], ring[2]]
        R_OUT = [ring[2], ring[0]]
        ctx_ps = ctx_bank[:, 0:HEADS * V1].rearrange("p (h d) -> p h d", h=HEADS)

        w_in = [sem(f"w_in{n}") for n in range(4)]
        small_in = sem("small_in")
        x_loaded = [sem(f"x_loaded{p}") for p in range(2)]
        adj_loaded = [sem(f"adj_loaded{p}") for p in range(2)]
        heads_placed = [sem(f"heads_placed{j}") for j in range(C)]
        out_stored = [sem(f"out_stored{t}") for t in range(QT)]
        dve_chain = sem("dve_chain")
        pool_const = sem("pool_const")
        peak_ready = sem("peak_ready")
        peaks_joined = sem("peaks_joined")
        scales_ready = sem("scales_ready")
        factors_ready = sem("factors_ready")
        wide_ready = sem("wide_ready")
        w_hi_ready = sem("w_hi_ready")
        w_lo_ready = sem("w_lo_ready")
        bias_ps_ready = sem("bias_ps_ready")
        bf_ready = sem("bf_ready")
        ones_ready = sem("ones_ready")
        passed = sem("passed")
        moments = sem("moments")
        var_ready = sem("var_ready")
        rstd_ready = sem("rstd_ready")
        norm_ready = sem("norm_ready")
        mask_ready = sem("mask_ready")
        residual_ready = sem("residual_ready")
        ht_ready = sem("ht_ready")
        h_hi_ready = sem("h_hi_ready")
        h_lo_ready = sem("h_lo_ready")
        qk_ready = sem("qk_ready")
        qk32_ready = sem("qk32_ready")
        qk_hi_ready = sem("qk_hi_ready")
        qk_lo_ready = sem("qk_lo_ready")
        v_ready = sem("v_ready")
        v_hi_ready = sem("v_hi_ready")
        v_lo_ready = sem("v_lo_ready")
        scores_ready = sem("scores_ready")
        logits_ready = sem("logits_ready")
        probs_ready = sem("probs_ready")
        pt_ready = sem("pt_ready")
        pt_hi_ready = sem("pt_hi_ready")
        pt_lo_ready = sem("pt_lo_ready")
        ctx_ready = sem("ctx_ready")
        inv_ready = sem("inv_ready")
        context_ready = sem("context_ready")
        ct_ready = sem("ct_ready")
        ct_hi_ready = sem("ct_hi_ready")
        ct_lo_ready = sem("ct_lo_ready")
        out_ready = sem("out_ready")
        result_ready = sem("result_ready")

        class Batch:

            def __init__(self, i, k):
                self.i, self.k, self.parity = i, k, k % 2

            def __add__(self, n):
                return Batch(self.i, self.k + n)

            def exists(self):
                return not isinstance(self.i, int) or 0 <= self.k < B

            def index(self):
                return self.i * 2 + self.k

            def count(self, per, extra=0):
                return self.i * (2 * per) + (self.k * per + extra)

            def dma_count(self, per=1):
                return self.i * (16 * per) + (self.k // 2 + 1) * 16 * per

        def wait(eng, s, value):
            if not isinstance(value, int) or value > 0:
                eng.wait_ge(s, value)

        PAIRS_BEFORE_LOOP = 1
        TURNS = (B - 4) // 2
        assert PAIRS_BEFORE_LOOP == 1 and TURNS > 0

        def alone(eng):
            eng.sem_inc(passed, 1)

        def cycles(eng, cycle):
            for k in (-1, 0):
                cycle(Batch(0, k))
            with eng.Fori(0, TURNS) as i:
                cycle(Batch(i, 1))
                cycle(Batch(i, 2))
            for k in range(2 * TURNS + 1, B + 1):
                cycle(Batch(0, k))

        x_v = x.rearrange("b (t p) h -> b p t h", p=P)
        adj_v = adj.rearrange("b (t p) k -> b p t k", p=P)
        out_v = out.rearrange("b (t p) h -> b t p h", p=P)
        block = ctx.enter_context(nc.Block())

        @block.sync
        def _(sp):
            def load_x(b):
                sp.dma_start(x_in[b.parity][:], x_v[b.index()]).then_inc(x_loaded[b.parity], 16)

            def load_adj(b):
                sp.dma_start(adj_in[b.parity][:], adj_v[b.index()]).then_inc(adj_loaded[b.parity], 16)

            def store(b, t):
                wait(sp, result_ready, b.count(2, t + 1))
                sp.dma_start(out_v[b.index(), t], result[t][:]).then_inc(out_stored[t], 16)

            def place_heads(b, j):
                wait(sp, qk_hi_ready, b.count(C, j + 1))
                wait(sp, qk_lo_ready, b.count(C, j + 1))
                for a in range(2):
                    own = slice(D * a, D * a + D)
                    other = slice(D - D * a, 2 * D - D * a)
                    dst, src = heads[b.parity][:, 2 * j + a], split[j]
                    sp.dma_start(dst[own, :, :], src[own, 1:4, :]).then_inc(heads_placed[j], 16)
                    sp.dma_start(dst[other, 0, :], src[own, 0, :]).then_inc(heads_placed[j], 16)
                    sp.dma_start(dst[other, 1:3, :], src[own, 2:4, :]).then_inc(heads_placed[j], 16)

            def load_w(n, W):
                sp.dma_start(w_raw[:, n], W.rearrange("(c p) n -> p c n", p=P)).then_inc(w_in[n], 16)

            def load_column(dst, src):
                sp.dma_start(dst, src.rearrange("(c p) -> p c", p=P),
                             allow_slow_non_contiguous=True).then_inc(small_in, 16)

            load_x(Batch(0, 0))
            load_w(0, Wq)
            load_w(1, Wk)
            load_column(qk_bias[:, 0], bq)
            load_column(qk_bias[:, 1], bk)
            load_column(bv_col[:], bv)
            sp.dma_start(bf_row[:], bf.rearrange("(a n) -> a n", a=1)).then_inc(small_in, 16)
            load_w(3, Wf)
            load_w(2, Wv)
            load_adj(Batch(0, 0))
            load_x(Batch(0, 1))
            load_adj(Batch(0, 1))

            def cycle(b):
                if (b + -1).exists():
                    store(b + -1, 0)
                if (b + 3).exists() and (b + 1).exists():
                    wait(sp, mask_ready, (b + 1).count(2, 2))
                    load_adj(b + 3)
                if (b + 1).exists():
                    place_heads(b + 1, 0)
                    place_heads(b + 1, 1)
                if (b + -1).exists():
                    store(b + -1, 1)
                if (b + 3).exists() and (b + 1).exists():
                    wait(sp, residual_ready, (b + 1).count(2, 2))
                    load_x(b + 3)
                if (b + 1).exists():
                    place_heads(b + 1, 2)

            cycles(sp, cycle)
            for t in range(QT):
                sp.wait_ge(out_stored[t], 16 * B)

        @block.gpsimd
        def _(pool):
            def normalise(b):
                wait(pool, var_ready, b.count(2, 2))
                pool.tensor_tensor(rstd[:], var_s[:], half[:], ALU.pow).then_inc(rstd_ready, 1)
                pool.wait_ge(rstd_ready, b.count(1, 1))
                wait(pool, ht_ready, b.count(2, 0))
                alone(pool)
                for t in range(QT):
                    pool.tensor_scalar(normed[:, t], x_in[b.parity][:, t], neg_mean[:, t:t + 1],
                                       rstd[:, t:t + 1], ALU.add, ALU.mult).then_inc(norm_ready, 1)

            def make_mask(b):
                wait(pool, adj_loaded[b.parity], b.dma_count())
                wait(pool, logits_ready, (b + -1).count(2 * UNITS, 0))
                alone(pool)
                for t in range(QT):
                    pool.tensor_scalar(mask[b.parity][:, t], adj_in[b.parity][:, t], -1.0,
                                       mask_scale[:, 0:1], ALU.add, ALU.mult).then_inc(mask_ready, 1)

            def split_lo(b, j):
                wait(pool, qk_hi_ready, b.count(C, j + 1))
                pool.tensor_tensor(split[j][:, 0:4:3, :], qk32[j][:], split[j][:, 1:3, :],
                                   ALU.subtract).then_inc(qk_lo_ready, 1)

            def add_bias(b):
                wait(pool, x_loaded[b.parity], b.dma_count())
                wait(pool, result_ready, (b + -1).count(2, 0))
                for t in range(QT):
                    pool.tensor_tensor(residual[b.parity][:, t], x_in[b.parity][:, t], bf_full[:],
                                       ALU.add).then_inc(residual_ready, 1)

            pool.memset(ident[:], 0.0).then_inc(pool_const, 1)
            pool.memset(half[:], -0.5).then_inc(pool_const, 1)
            pool.memset(ones_row[:], 1.0).then_inc(pool_const, 1)
            pool.wait_ge(pool_const, 3)
            pool.affine_select(out=ident[:], in_=ident[:], compare_op=ALU.not_equal, fill=1.0, base=0,
                               pattern=[[-1, P]], channel_multiplier=1).then_inc(pool_const, 1)
            normalise(Batch(0, 0))
            pool.wait_ge(peak_ready, 4)
            pool.partition_all_reduce(qk_peak_all[:], qk_peak[:], P, ALL_MAX).then_inc(peaks_joined, 1)
            pool.wait_ge(peak_ready, 6)
            pool.partition_all_reduce(vf_peak_all[:], vf_peak[:], P, ALL_MAX).then_inc(peaks_joined, 1)
            pool.wait_ge(factors_ready, 1)

            def cycle(b):
                if (b + 1).exists():
                    make_mask(b + 1)
                    split_lo(b + 1, 0)
                    split_lo(b + 1, 1)
                    if b.k == -1:
                        pool.wait_ge(bf_ready, 1)
                    add_bias(b + 1)
                if (b + 2).exists():
                    normalise(b + 2)
                if (b + 1).exists():
                    split_lo(b + 1, 2)

            cycles(pool, cycle)

        @block.scalar
        def _(act):
            def exps(b, u):
                for a in range(2):
                    wait(act, logits_ready, b.count(2 * UNITS, 2 * u + a + 1))
                    act.activation(probs[u % 2][:, a], logits[u % 2][:, a], ACT.Exp,
                                   bias=least[u % 2][:, a:a + 1], scale=-1.0).then_inc(probs_ready, 1)

            def probs_hi(b, u):
                wait(act, pt_ready, b.count(UNITS, u + 1))
                act.activation(pt_hi[u % 2][:].rearrange("p a t q -> p (a t q)"), pt_bank[u % 2][:],
                               ACT.Copy, scale=P_SCALE).then_inc(pt_hi_ready, 1)

            def h_hi_part(b):
                for n, (c0, c1, src) in enumerate(((0, 2, R_HT[0]), (2, 3, R_HT[1]))):
                    wait(act, ht_ready, b.count(2, n + 1))
                    act.activation(h_hi[:, c0:c1].rearrange("p c s -> p (c s)"),
                                   src[:, 0:(c1 - c0) * S], ACT.Relu).then_inc(h_hi_ready, 1)

            def qk_full(b, j):
                wait(act, qk_ready, b.count(C, j + 1))
                for n in range(2):
                    act.activation(qk32[j][:, n], R_QK[j][:, n * S:(n + 1) * S], ACT.Identity,
                                   bias=qk_bias_s[:, n, j:j + 1], scale=qk_ratio[:, n:n + 1])\
                       .then_inc(qk32_ready, 1)

            def v_hi_part(b, t):
                wait(act, v_ready, b.count(2, t + 1))
                act.activation(v_hi[b.parity][:, t, :, 0:D], R_V[t][:, 0:H].rearrange("p (h d) -> p h d", d=D),
                               ACT.Copy, scale=v_ratio[:, 0:1]).then_inc(v_hi_ready, 1)

            def context_hi(b, t):
                wait(act, ct_ready, b.count(2, t + 1))
                act.activation(ct_hi[t][:].rearrange("p c q -> p (c q)"), R_CT[t][:, 0:H],
                               ACT.Copy).then_inc(ct_hi_ready, 1)

            def weights_hi(n):
                col = (qk_scale, vf_scale)[n // 2][:, n % 2:n % 2 + 1]
                act.activation(w_hi[:, n].rearrange("p c n -> p (c n)"), w_raw[:, n].rearrange("p c n -> p (c n)"),
                               ACT.Copy, scale=col).then_inc(w_hi_ready, 1)

            act.wait_ge(scales_ready, 1)
            weights_hi(0)
            weights_hi(1)
            h_hi_part(Batch(0, 0))
            act.wait_ge(scales_ready, 2)
            weights_hi(2)
            weights_hi(3)
            act.wait_ge(factors_ready, 1)

            def cycle(b):
                here, before, front = b.exists(), (b + -1).exists(), (b + 1).exists()

                def hi_of(u):
                    if u == 0:
                        if before:
                            probs_hi(b + -1, UNITS - 1)
                    elif here:
                        probs_hi(b, u - 1)

                hi_of(0)
                if front and b.k != -1:
                    h_hi_part(b + 1)
                if here:
                    exps(b, 0)
                hi_of(1)
                if here:
                    exps(b, 1)
                if front:
                    qk_full(b + 1, 0)
                hi_of(2)
                if here:
                    exps(b, 2)
                if front:
                    qk_full(b + 1, 1)
                if before:
                    context_hi(b + -1, 1)
                hi_of(3)
                if here:
                    exps(b, 3)
                hi_of(4)
                if here:
                    exps(b, 4)
                if front:
                    qk_full(b + 1, 2)
                    if b.k == -1:
                        act.wait_ge(factors_ready, 2)
                    v_hi_part(b + 1, 0)
                hi_of(5)
                if here:
                    exps(b, 5)
                if front:
                    v_hi_part(b + 1, 1)
                if here:
                    context_hi(b, 0)

            cycles(act, cycle)

        @block.vector
        def _(dve):
            chain = [0]

            def step(instruction):
                chain[0] += 1
                instruction.then_inc(dve_chain, 1)
                dve.wait_ge(dve_chain, chain[0])

            def mask_and_max(b, u):
                t, j = u // C, u % C
                wait(dve, scores_ready, b.count(UNITS, u + 1))
                if u == 0:
                    wait(dve, mask_ready, b.count(2, 2))
                alone(dve)
                for a in range(2):
                    dve.tensor_tensor_reduce(
                        out=logits[u % 2][:, a], in0=score_bank[u % 2][:, a * S:(a + 1) * S],
                        in1=mask[b.parity][:, t], scale=logit_unscale[:, 0:1], scalar=FAR,
                        op0=ALU.add, op1=ALU.min, accum_out=least[u % 2][:, a:a + 1]).then_inc(logits_ready, 1)

            def probs_lo(b, u):
                wait(dve, pt_hi_ready, b.count(UNITS, u + 1))
                dve.scalar_tensor_tensor(
                    out=pt_lo[u % 2][:].rearrange("p a t q -> p (a t q)"), in0=pt_bank[u % 2][:],
                    scalar=P_SCALE, in1=pt_hi[u % 2][:].rearrange("p a t q -> p (a t q)"),
                    op0=ALU.mult, op1=ALU.subtract).then_inc(pt_lo_ready, 1)

            def h_lo_part(b):
                for n, (c0, c1, src) in enumerate(((0, 2, R_HT[0]), (2, 3, R_HT[1]))):
                    wait(dve, h_hi_ready, b.count(2, n + 1))
                    dve.scalar_tensor_tensor(
                        out=h_lo[:, c0:c1].rearrange("p c s -> p (c s)"), in0=src[:, 0:(c1 - c0) * S],
                        scalar=0.0, in1=h_hi[:, c0:c1].rearrange("p c s -> p (c s)"),
                        op0=ALU.max, op1=ALU.subtract).then_inc(h_lo_ready, 1)

            def qk_hi_part(b, j):
                wait(dve, qk32_ready, b.count(2 * C, 2 * j + 2))
                dve.tensor_copy(split[j][:, 1:3], qk32[j][:]).then_inc(qk_hi_ready, 1)

            def v_lo_part(b, t):
                wait(dve, v_hi_ready, b.count(2, t + 1))
                dve.scalar_tensor_tensor(
                    out=v_lo[b.parity][:, t], in0=R_V[t][:, 0:H].rearrange("p (h d) -> p h d", d=D),
                    scalar=v_ratio[:, 0:1], in1=v_hi[b.parity][:, t, :, 0:D],
                    op0=ALU.mult, op1=ALU.subtract).then_inc(v_lo_ready, 1)

            def divide(b, t):
                wait(dve, ctx_ready, b.count(UNITS, C * (t + 1)))
                dve.reciprocal(inv_sum[t][:], ctx_ps[:, :, D]).then_inc(inv_ready, 1)
                dve.wait_ge(inv_ready, b.count(2, t + 1))
                dve.tensor_tensor(context[t][:], ctx_ps[:, :, 0:D],
                                  inv_sum[t][:].unsqueeze(2).to_broadcast([P, HEADS, D]),
                                  ALU.mult).then_inc(context_ready, 1)

            def context_lo(b, t):
                wait(dve, ct_hi_ready, b.count(2, t + 1))
                dve.tensor_tensor(ct_lo[t][:].rearrange("p c q -> p (c q)"), R_CT[t][:, 0:H],
                                  ct_hi[t][:].rearrange("p c q -> p (c q)"),
                                  ALU.subtract).then_inc(ct_lo_ready, 1)

            def finish(b, t):
                wait(dve, out_ready, b.count(2, t + 1))
                wait(dve, residual_ready, b.count(2, t + 1))
                wait(dve, out_stored[t], b.count(16, 0))
                dve.scalar_tensor_tensor(out=result[t][:], in0=R_OUT[t][:, 0:H], scalar=out_unscale[:, 0:1],
                                         in1=residual[b.parity][:, t], op0=ALU.mult,
                                         op1=ALU.add).then_inc(result_ready, 1)

            def layer_stats(b):
                wait(dve, x_loaded[b.parity], b.dma_count())
                for t in range(QT):
                    dve.bn_stats(out=stats[:, t], in_=x_in[b.parity][:, t]).then_inc(moments, 1)
                for t in range(QT):
                    dve.wait_ge(moments, b.count(4, t + 1))
                    alone(dve)
                    dve.bn_aggr(out=mean_var[:, t], in_=stats[:, t]).then_inc(moments, 1)
                dve.wait_ge(moments, b.count(4, 4))
                wait(dve, norm_ready, b.count(2, 0))
                dve.tensor_scalar(var_s[:], mean_var[:, :, 1], EPS, H_SCALE ** -2, ALU.add,
                                  ALU.mult).then_inc(var_ready, 1)
                dve.tensor_scalar(neg_mean[:], mean_var[:, :, 0], -1.0, None,
                                  ALU.mult).then_inc(var_ready, 1)

            def weight_peak(n, out):
                dve.wait_ge(w_in[n], 16)
                dve.tensor_reduce(out, w_raw[:, n].rearrange("p c n -> p (c n)"), AX_X, ALU.max,
                                  apply_absolute_value=True).then_inc(peak_ready, 1)

            def powers(bounds, scales, unscales):
                step(dve.tensor_scalar(bounds[:].bitcast(I32), bounds[:].bitcast(I32), EXPONENT, None,
                                       ALU.bitwise_and))
                step(dve.tensor_scalar(unscales[:], bounds[:], 1.0 / TOP, None, ALU.mult))
                step(dve.reciprocal(scales[:], unscales[:]))

            def weights_lo(n):
                dve.wait_ge(w_hi_ready, n + 1)
                col = (qk_scale, vf_scale)[n // 2][:, n % 2:n % 2 + 1]
                dve.scalar_tensor_tensor(
                    out=w_lo[:, n].rearrange("p c n -> p (c n)"), in0=w_raw[:, n].rearrange("p c n -> p (c n)"),
                    scalar=col, in1=w_hi[:, n].rearrange("p c n -> p (c n)"),
                    op0=ALU.mult, op1=ALU.subtract).then_inc(w_lo_ready, 1)

            step(dve.memset(zeros[:], 0.0))
            for p in range(2):
                dve.memset(v_hi[p][:, :, :, D:V1], 1.0).then_inc(ones_ready, 1)
            layer_stats(Batch(0, 0))
            weight_peak(0, qk_peak[:, 0:1])
            weight_peak(1, qk_peak[:, 1:2])
            dve.wait_ge(small_in, 64)
            for n in range(2):
                dve.tensor_reduce(qk_peak[:, 2 + n:3 + n], qk_bias[:, n], AX_X, ALU.max,
                                  apply_absolute_value=True).then_inc(peak_ready, 1)
            for c in range(C):
                dve.tensor_scalar(bv_wide[:, c], zeros[:], bv_col[:, c:c + 1], None,
                                  ALU.add).then_inc(wide_ready, 1)
            dve.wait_ge(peaks_joined, 1)
            step(dve.tensor_scalar(qk_bound[:, 0:2], qk_peak_all[:, 0:2], LEAST, None, ALU.max))
            step(dve.scalar_tensor_tensor(out=qk_bound[:, 2:4], in0=qk_peak_all[:, 0:2], scalar=float(H),
                                          in1=qk_peak_all[:, 2:4], op0=ALU.mult, op1=ALU.add))
            step(dve.tensor_scalar(qk_bound[:, 2:4], qk_bound[:, 2:4], LEAST_QK, None, ALU.max))
            powers(qk_bound, qk_scale, qk_unscale)
            dve.tensor_copy(zeros[:, 0:1], qk_scale[:, 0:1]).then_inc(scales_ready, 1)
            step(dve.scalar_tensor_tensor(out=qk_ratio[:], in0=qk_scale[:, 2:4], scalar=1.0 / H_SCALE,
                                          in1=qk_unscale[:, 0:2], op0=ALU.mult, op1=ALU.mult))
            step(dve.tensor_tensor(logit_product[:, 0:1], qk_unscale[:, 2:3], qk_unscale[:, 3:4], ALU.mult))
            step(dve.tensor_tensor(logit_product[:, 1:2], qk_scale[:, 2:3], qk_scale[:, 3:4], ALU.mult))
            step(dve.tensor_scalar(logit_unscale[:], logit_product[:, 0:1], -1.0 / D ** 0.5, None, ALU.mult))
            step(dve.tensor_scalar(mask_scale[:], logit_product[:, 1:2], -NEG * D ** 0.5, None, ALU.mult))
            step(dve.tensor_scalar(qk_bias_s[:, 0], qk_bias[:, 0], qk_scale[:, 2:3], None, ALU.mult))
            dve.tensor_scalar(qk_bias_s[:, 1], qk_bias[:, 1], qk_scale[:, 3:4], None,
                              ALU.mult).then_inc(factors_ready, 1)
            weights_lo(0)
            weights_lo(1)
            h_lo_part(Batch(0, 0))
            weight_peak(2, vf_peak[:, 0:1])
            weight_peak(3, vf_peak[:, 1:2])
            dve.wait_ge(bias_ps_ready, 1)
            dve.tensor_copy(bf_full[:], ctx_bank[:, 0:H]).then_inc(bf_ready, 1)
            dve.wait_ge(peaks_joined, 2)
            step(dve.tensor_copy(vf_bound[:, 0:2], vf_peak_all[:]))
            step(dve.tensor_scalar(vf_bound[:, 2:3], vf_peak_all[:, 0:1], float(H), None, ALU.mult))
            step(dve.tensor_scalar(vf_bound[:], vf_bound[:], LEAST, None, ALU.max))
            powers(vf_bound, vf_scale, vf_unscale)
            dve.tensor_copy(zeros[:, 0:1], vf_scale[:, 0:1]).then_inc(scales_ready, 1)
            step(dve.scalar_tensor_tensor(out=v_ratio[:], in0=vf_scale[:, 2:3], scalar=1.0 / H_SCALE,
                                          in1=vf_unscale[:, 0:1], op0=ALU.mult, op1=ALU.mult))
            step(dve.tensor_tensor(out_unscale[:], vf_unscale[:, 2:3], vf_unscale[:, 1:2], ALU.mult))
            dve.tensor_copy(zeros[:, 1:2], v_ratio[:]).then_inc(factors_ready, 1)
            weights_lo(2)
            weights_lo(3)

            def cycle(b):
                here, before, front = b.exists(), (b + -1).exists(), (b + 1).exists()

                def lo_of(u):
                    if u == 0:
                        if before:
                            probs_lo(b + -1, UNITS - 1)
                    elif here:
                        probs_lo(b, u - 1)

                if here:
                    mask_and_max(b, 0)
                lo_of(0)
                if front and b.k != -1:
                    h_lo_part(b + 1)
                if before:
                    finish(b + -1, 0)
                if here:
                    mask_and_max(b, 1)
                lo_of(1)
                if front:
                    qk_hi_part(b + 1, 0)
                if before:
                    divide(b + -1, 1)
                if here:
                    mask_and_max(b, 2)
                lo_of(2)
                if front:
                    qk_hi_part(b + 1, 1)
                if before:
                    context_lo(b + -1, 1)
                if here:
                    mask_and_max(b, 3)
                lo_of(3)
                if (b + 2).exists():
                    layer_stats(b + 2)
                if before:
                    finish(b + -1, 1)
                if here:
                    mask_and_max(b, 4)
                lo_of(4)
                if front:
                    qk_hi_part(b + 1, 2)
                    v_lo_part(b + 1, 0)
                if here:
                    divide(b, 0)
                if here:
                    mask_and_max(b, 5)
                lo_of(5)
                if front:
                    v_lo_part(b + 1, 1)
                if here:
                    context_lo(b, 0)

            cycles(dve, cycle)

        @block.tensor
        def _(pe):
            def three(out_ap, a_hi, a_lo, m_hi, m_lo, first, last):
                pe.matmul(out_ap, a_hi, m_hi, start=first, stop=False)
                pe.matmul(out_ap, a_hi, m_lo, start=False, stop=False)
                return pe.matmul(out_ap, a_lo, m_hi, start=False, stop=last)

            def transpose_h(b):
                for t in range(QT):
                    wait(pe, norm_ready, b.count(2, t + 1))
                for n, (c0, c1, dst) in enumerate(((0, 2, R_HT[0]), (2, 3, R_HT[1]))):
                    wait(pe, v_lo_ready, (b + -1).count(2, n + 1))
                    for c in range(c0, c1):
                        for t in range(QT):
                            o = (c - c0) * S + t * P
                            mm = pe.transpose(dst[:, o:o + P], normed[:, t, c * P:(c + 1) * P], ident[:])
                    mm.then_inc(ht_ready, 1)

            def project_qk(b, j, parts=(0, 1)):
                if j == 0:
                    wait(pe, h_lo_ready, b.count(2, 2))
                if j == 2 and 0 in parts:
                    wait(pe, qk32_ready, b.count(2 * C, 4))
                for n in parts:
                    for c in range(C):
                        col = slice(j * P, (j + 1) * P)
                        mm = three(R_QK[j][:, n * S:(n + 1) * S], w_hi[:, n, c, col], w_lo[:, n, c, col],
                                   h_hi[:, c], h_lo[:, c], c == 0, c == C - 1)
                if 1 in parts:
                    mm.then_inc(qk_ready, 1)

            def project_v(b, t):
                if t == 0:
                    if (b + -2).exists():
                        wait(pe, result_ready, (b + -2).count(2, 2))
                else:
                    wait(pe, qk32_ready, b.count(2 * C, 6))
                for c in range(C):
                    tok = slice(t * P, (t + 1) * P)
                    mm = three(R_V[t][:, 0:H], h_hi[:, c, tok], h_lo[:, c, tok],
                               w_hi[:, 2, c], w_lo[:, 2, c], c == 0, c == C - 1)
                mm.then_inc(v_ready, 1)

            def scores(b, u):
                t, j = u // C, u % C
                if t == 0:
                    wait(pe, heads_placed[j], b.count(6 * 16, 6 * 16))
                wait(pe, logits_ready, b.count(2 * UNITS, 2 * u - 2))
                for a in range(2):
                    h = heads[b.parity][:, 2 * j + a]
                    q = h[:, 0, t * P:(t + 1) * P]
                    o = score_bank[u % 2][:, a * S:(a + 1) * S]
                    pe.matmul(o, q, h[:, 1], start=True, stop=False)
                    mm = pe.matmul(o, q, h[:, 2], start=False, stop=True)
                mm.then_inc(scores_ready, 1)

            def transpose_probs(b, u):
                wait(pe, pt_lo_ready, b.count(UNITS, u - 1))
                for a in range(2):
                    wait(pe, probs_ready, b.count(2 * UNITS, 2 * u + a + 1))
                    for s in range(QT):
                        o = (a * QT + s) * P
                        mm = pe.transpose(pt_bank[u % 2][:, o:o + P], probs[u % 2][:, a, s * P:(s + 1) * P],
                                          ident[:])
                mm.then_inc(pt_ready, 1)

            def apply_probs(b, u):
                t, j = u // C, u % C
                wait(pe, pt_lo_ready, b.count(UNITS, u + 1))
                if u == 0:
                    wait(pe, v_lo_ready, b.count(2, 2))
                if j == 0:
                    wait(pe, context_ready, b.count(2, t))
                for a in range(2):
                    h = 2 * j + a
                    for s in range(QT):
                        hi, lo = pt_hi[u % 2][:, a, s], pt_lo[u % 2][:, a, s]
                        vh, vl = v_hi[b.parity][:, s, h], v_lo[b.parity][:, s, h]
                        pe.matmul(ctx_ps[:, h], hi, vh, start=(s == 0), stop=False)
                        pe.matmul(ctx_ps[:, h, 0:D], hi, vl, start=False, stop=False)
                        mm = pe.matmul(ctx_ps[:, h], lo, vh, start=False, stop=(s == QT - 1))
                mm.then_inc(ctx_ready, 1)

            def transpose_context(b, t):
                wait(pe, context_ready, b.count(2, t + 1))
                if t == 1:
                    wait(pe, result_ready, b.count(2, 1))
                for c in range(C):
                    mm = pe.transpose(R_CT[t][:, c * P:(c + 1) * P],
                                      context[t][:, 2 * c:2 * c + 2].rearrange("p h d -> p (h d)"), ident[:])
                mm.then_inc(ct_ready, 1)

            def project_out(b, t):
                wait(pe, ct_lo_ready, b.count(2, t + 1))
                if t == 1 and (b + 2).exists():
                    wait(pe, qk32_ready, (b + 2).count(2 * C, 2))
                for c in range(C):
                    mm = three(R_OUT[t][:, 0:H], ct_hi[t][:, c], ct_lo[t][:, c],
                               w_hi[:, 3, c], w_lo[:, 3, c], c == 0, c == C - 1)
                mm.then_inc(out_ready, 1)

            pe.wait_ge(pool_const, 4)
            transpose_h(Batch(0, 0))
            pe.wait_ge(small_in, 64)
            pe.wait_ge(wide_ready, C)
            pe.wait_ge(w_in[3], 16)
            pe.matmul(ctx_bank[:, 0:H], ones_row[:], bf_row[:], start=True, stop=False)
            for c in range(C):
                mm = pe.matmul(ctx_bank[:, 0:H], bv_wide[:, c], w_raw[:, 3, c], start=False, stop=(c == C - 1))
            mm.then_inc(bias_ps_ready, 1)

            def cycle(b):
                here, before, front = b.exists(), (b + -1).exists(), (b + 1).exists()

                def transpose_of(u):
                    if u == 0:
                        if before:
                            transpose_probs(b + -1, UNITS - 1)
                    elif here:
                        transpose_probs(b, u - 1)

                def apply_of(u):
                    if u < 2:
                        if before:
                            apply_probs(b + -1, UNITS - 2 + u)
                    elif here:
                        apply_probs(b, u - 2)

                transpose_of(0)
                if here:
                    scores(b, 0)
                if front and b.k != -1:
                    transpose_h(b + 1)
                apply_of(0)
                if before:
                    project_out(b + -1, 0)
                transpose_of(1)
                if here:
                    scores(b, 1)
                if front:
                    if b.k == -1:
                        pe.wait_ge(w_lo_ready, 2)
                    project_qk(b + 1, 0)
                apply_of(1)
                transpose_of(2)
                if here:
                    scores(b, 2)
                if front:
                    project_qk(b + 1, 1)
                if before:
                    transpose_context(b + -1, 1)
                apply_of(2)
                transpose_of(3)
                if here:
                    scores(b, 3)
                if front:
                    project_qk(b + 1, 2, (0,))
                if before:
                    project_out(b + -1, 1)
                apply_of(3)
                transpose_of(4)
                if here:
                    scores(b, 4)
                if front:
                    project_qk(b + 1, 2, (1,))
                    if b.k == -1:
                        pe.wait_ge(w_lo_ready, 4)
                        pe.wait_ge(bf_ready, 1)
                        pe.wait_ge(ones_ready, 2)
                    project_v(b + 1, 0)
                apply_of(4)
                transpose_of(5)
                if here:
                    scores(b, 5)
                if front:
                    project_v(b + 1, 1)
                if here:
                    transpose_context(b, 0)
                apply_of(5)

            cycles(pe, cycle)


_INS = ['x', 'adj', 'L0_gnn_Wq', 'L0_gnn_bq', 'L0_gnn_Wk', 'L0_gnn_bk', 'L0_gnn_Wv', 'L0_gnn_bv',
        'L0_gnn_Wf', 'L0_gnn_bf']


def kernel(**inputs):
    import numpy as _np
    import concourse.bacc as _bacc
    from concourse import mybir as _mybir
    from concourse.bass_utils import run_bass_kernel_spmd as _run

    nc = _bacc.Bacc("TRN2", target_bir_lowering=False, num_devices=1)
    arrays, args = {}, []
    for name in _INS:
        a = _np.ascontiguousarray(inputs[name])
        arrays[f"in_{name}_dram"] = a
        args.append(nc.dram_tensor(f"in_{name}_dram", a.shape, _mybir.dt.from_np(a.dtype), kind="ExternalInput").ap())
    args.append(nc.dram_tensor("out_0_dram", inputs['x'].shape, F32, kind="ExternalOutput").ap())
    gnn_attention(nc, *args)
    r = _run(nc, [arrays], core_ids=[0])
    return r.results[0]["out_0_dram"]
```

```python
from contextlib import ExitStack

import concourse.bass as bass
from concourse import mybir

F32 = mybir.dt.float32
F16 = mybir.dt.float16
I32 = mybir.dt.int32
ALU = mybir.AluOpType
ACT = mybir.ActivationFunctionType
AX_X = mybir.AxisListType.X
ALL_MAX = bass.bass_isa.ReduceOp.max

P = 128
HEADS = 6
EPS = 1e-5
NEG = -9000000000000000.0
H_SCALE = 2.0 ** 10
P_SCALE = 2.0 ** 14
TOP = 2.0 ** 14
LEAST = 2.0 ** -60
LEAST_QK = 2.0 ** -10
EXPONENT = 0x7F800000
WARM_UPS = 22
FAR = 3.0e38


def gnn_attention(nc, x, adj, Wq, bq, Wk, bk, Wv, bv, Wf, bf, out):
    B, S, H = x.shape
    D = H // HEADS
    C = H // P
    QT = S // P
    V1 = D + 1
    UNITS = QT * C
    assert D * 2 == P and QT == 2 and C == 3 and B % 2 == 0

    ctx = ExitStack()
    with ctx:
        def sb(name, shape, dt):
            return ctx.enter_context(nc.sbuf_tensor(name, shape, dt))

        def bank(name):
            return ctx.enter_context(nc.psum_tensor(name, [P, 512], F32))

        def sem(name):
            return ctx.enter_context(nc.semaphore(name))

        w_raw = sb("w_raw", [P, 4, C, H], F32)
        w_hi = sb("w_hi", [P, 4, C, H], F16)
        w_lo = sb("w_lo", [P, 4, C, H], F16)
        qk_bias = sb("qk_bias", [P, 2, C], F32)
        qk_bias_s = sb("qk_bias_s", [P, 2, C], F32)
        bv_col = sb("bv_col", [P, C], F32)
        bv_wide = sb("bv_wide", [P, C, P], F32)
        bf_row = sb("bf_row", [1, H], F32)
        ones_row = sb("ones_row", [1, P], F32)
        bf_full = sb("bf_full", [P, H], F32)
        zeros = sb("zeros", [P, P], F32)
        ident = sb("ident", [P, P], F32)
        half = sb("half", [P, QT], F32)
        qkv_peak = sb("qkv_peak", [P, 6], F32)
        qkv_peak_all = sb("qkv_peak_all", [P, 6], F32)
        qkv_bound = sb("qkv_bound", [P, 6], F32)
        qkv_scale = sb("qkv_scale", [P, 6], F32)
        qkv_unscale = sb("qkv_unscale", [P, 6], F32)
        f_peak = sb("f_peak", [P, 1], F32)
        f_peak_all = sb("f_peak_all", [P, 1], F32)
        f_bound = sb("f_bound", [P, 1], F32)
        f_scale = sb("f_scale", [P, 1], F32)
        f_unscale = sb("f_unscale", [P, 1], F32)
        qkv_ratio = sb("qkv_ratio", [P, 3], F32)
        logit_product = sb("logit_product", [P, 2], F32)
        logit_unscale = sb("logit_unscale", [P, 1], F32)
        mask_scale = sb("mask_scale", [P, 1], F32)
        out_unscale = sb("out_unscale", [P, 1], F32)

        x_in = [sb(f"x_in{p}", [P, QT, H], F32) for p in range(2)]
        adj_in = [sb(f"adj_in{p}", [P, QT, S], adj.dtype) for p in range(2)]
        residual = [sb(f"residual{p}", [P, QT, H], F32) for p in range(2)]
        mask = [sb(f"mask{p}", [P, QT, S], F32) for p in range(2)]
        stats = sb("stats", [P, QT, 6], F32)
        mean_var = sb("mean_var", [P, QT, 2], F32)
        var_s = sb("var_s", [P, QT], F32)
        neg_mean = sb("neg_mean", [P, QT], F32)
        rstd = sb("rstd", [P, QT], F32)
        normed = sb("normed", [P, QT, H], F32)
        h_hi = sb("h_hi", [P, C, S], F16)
        h_lo = sb("h_lo", [P, C, S], F16)
        qk32 = [sb(f"qk32_{j}", [P, 2, S], F32) for j in range(C)]
        split = [sb(f"split{j}", [P, 4, S], F16) for j in range(C)]
        heads = [sb(f"heads{p}", [P, HEADS, 3, S], F16) for p in range(2)]
        v_hi = [sb(f"v_hi{p}", [P, QT, HEADS, V1], F16) for p in range(2)]
        v_lo = [sb(f"v_lo{p}", [P, QT, HEADS, D], F16) for p in range(2)]
        logits = [sb(f"logits{u}", [P, 2, S], F32) for u in range(2)]
        least = [sb(f"least{u}", [P, 2], F32) for u in range(2)]
        probs = [sb(f"probs{u}", [P, 2, S], F32) for u in range(2)]
        pt_hi = [sb(f"pt_hi{u}", [P, 2, QT, P], F16) for u in range(2)]
        pt_lo = [sb(f"pt_lo{u}", [P, 2, QT, P], F16) for u in range(2)]
        inv_sum = [sb(f"inv_sum{t}", [P, HEADS], F32) for t in range(QT)]
        context = [sb(f"context{t}", [P, HEADS, D], F32) for t in range(QT)]
        ct_hi = [sb(f"ct_hi{t}", [P, C, P], F16) for t in range(QT)]
        ct_lo = [sb(f"ct_lo{t}", [P, C, P], F16) for t in range(QT)]
        result = [sb(f"result{t}", [P, H], F32) for t in range(QT)]

        score_bank = [bank("scores0"), bank("scores1")]
        pt_bank = [bank("probs_t0"), bank("probs_t1")]
        ctx_bank = bank("ctx")
        ring = [bank("ring0"), bank("ring1"), bank("ring2")]
        R_HT = ring[0:2]
        R_QK = [ring[0], ring[1], ring[1]]
        R_V = ring[0:2]
        R_CT = [ring[2], ring[2]]
        R_OUT = [ring[2], ring[0]]
        ctx_ps = ctx_bank[:, 0:HEADS * V1].rearrange("p (h d) -> p h d", h=HEADS)

        w_in = [sem(f"w_in{n}") for n in range(4)]
        small_in = sem("small_in")
        x_loaded = [sem(f"x_loaded{p}") for p in range(2)]
        adj_loaded = [sem(f"adj_loaded{p}") for p in range(2)]
        heads_placed = [sem(f"heads_placed{j}") for j in range(C)]
        out_stored = [sem(f"out_stored{t}") for t in range(QT)]
        zeros_placed = sem("zeros_placed")
        dve_chain = sem("dve_chain")
        pool_const = sem("pool_const")
        peak_ready = sem("peak_ready")
        peaks_joined = sem("peaks_joined")
        scales_ready = sem("scales_ready")
        factors_ready = sem("factors_ready")
        wide_ready = sem("wide_ready")
        w_hi_ready = sem("w_hi_ready")
        w_lo_ready = sem("w_lo_ready")
        bias_ps_ready = sem("bias_ps_ready")
        bf_ready = sem("bf_ready")
        ones_ready = sem("ones_ready")
        passed = sem("passed")
        moments = sem("moments")
        var_ready = sem("var_ready")
        rstd_ready = sem("rstd_ready")
        norm_ready = sem("norm_ready")
        mask_ready = sem("mask_ready")
        residual_ready = sem("residual_ready")
        ht_ready = sem("ht_ready")
        h_hi_ready = sem("h_hi_ready")
        h_lo_ready = sem("h_lo_ready")
        qk_ready = sem("qk_ready")
        qk32_ready = sem("qk32_ready")
        qk_hi_ready = sem("qk_hi_ready")
        qk_lo_ready = sem("qk_lo_ready")
        v_ready = sem("v_ready")
        v_hi_ready = sem("v_hi_ready")
        v_lo_ready = sem("v_lo_ready")
        scores_ready = sem("scores_ready")
        logits_ready = sem("logits_ready")
        probs_ready = sem("probs_ready")
        pt_ready = sem("pt_ready")
        pt_hi_ready = sem("pt_hi_ready")
        pt_lo_ready = sem("pt_lo_ready")
        ctx_ready = sem("ctx_ready")
        inv_ready = sem("inv_ready")
        context_ready = sem("context_ready")
        ct_ready = sem("ct_ready")
        ct_hi_ready = sem("ct_hi_ready")
        ct_lo_ready = sem("ct_lo_ready")
        out_ready = sem("out_ready")
        result_ready = sem("result_ready")

        class Batch:

            def __init__(self, i, k):
                self.i, self.k, self.parity = i, k, k % 2

            def __add__(self, n):
                return Batch(self.i, self.k + n)

            def exists(self):
                return not isinstance(self.i, int) or 0 <= self.k < B

            def index(self):
                return self.i * 2 + self.k

            def count(self, per, extra=0):
                assert isinstance(self.i, int) or self.k * per + extra > 0
                return self.i * (2 * per) + (self.k * per + extra)

            def dma_count(self, per=1):
                return self.i * (16 * per) + (self.k // 2 + 1) * 16 * per

        def wait(eng, s, value):
            if not isinstance(value, int) or value > 0:
                eng.wait_ge(s, value)

        TURNS = (B - 4) // 2
        assert TURNS > 0

        def pair(j):
            return slice(j * P, (j + 1) * P)

        def w_scale(n):
            return f_scale[:, 0:1] if n == 3 else qkv_scale[:, n:n + 1]

        def alone(eng):
            eng.sem_inc(passed, 1)

        def cycles(eng, cycle):
            for k in (-1, 0):
                cycle(Batch(0, k))
            with eng.Fori(0, TURNS) as i:
                cycle(Batch(i, 1))
                cycle(Batch(i, 2))
            for k in range(2 * TURNS + 1, B + 1):
                cycle(Batch(0, k))

        x_v = x.rearrange("b (t p) h -> b p t h", p=P)
        adj_v = adj.rearrange("b (t p) k -> b p t k", p=P)
        out_v = out.rearrange("b (t p) h -> b t p h", p=P)
        block = ctx.enter_context(nc.Block())

        @block.sync
        def _(sp):
            def load_x(b):
                sp.dma_start(x_in[b.parity][:], x_v[b.index()]).then_inc(x_loaded[b.parity], 16)

            def load_adj(b):
                sp.dma_start(adj_in[b.parity][:], adj_v[b.index()]).then_inc(adj_loaded[b.parity], 16)

            def store(b, t):
                wait(sp, result_ready, b.count(2, t + 1))
                sp.dma_start(out_v[b.index(), t], result[t][:]).then_inc(out_stored[t], 16)

            def place_heads(b, j):
                wait(sp, qk_hi_ready, b.count(C, j + 1))
                wait(sp, qk_lo_ready, b.count(C, j + 1))
                for a in range(2):
                    own = slice(D * a, D * a + D)
                    other = slice(D - D * a, 2 * D - D * a)
                    dst, src = heads[b.parity][:, 2 * j + a], split[j]
                    sp.dma_start(dst[own], src[own, 1:4]).then_inc(heads_placed[j], 16)
                    sp.dma_start(dst[other, 0:2], src[own, 0:3:2]).then_inc(heads_placed[j], 16)

            def load_w(n, W):
                sp.dma_start(w_raw[:, n], W.rearrange("(c p) n -> p c n", p=P)).then_inc(w_in[n], 16)

            def load_column(dst, src):
                sp.dma_start(dst, src.rearrange("(c p) -> p c", p=P),
                             allow_slow_non_contiguous=True).then_inc(small_in, 16)

            load_x(Batch(0, 0))
            load_w(0, Wq)
            load_w(1, Wk)
            load_column(qk_bias[:, 0], bq)
            load_column(qk_bias[:, 1], bk)
            load_column(bv_col[:], bv)
            sp.dma_start(bf_row[:], bf.rearrange("(a n) -> a n", a=1)).then_inc(small_in, 16)
            load_w(2, Wv)
            load_w(3, Wf)
            load_adj(Batch(0, 0))
            load_x(Batch(0, 1))
            load_adj(Batch(0, 1))

            def cycle(b):
                if (b + -1).exists():
                    store(b + -1, 0)
                if (b + 3).exists() and (b + 1).exists():
                    wait(sp, mask_ready, (b + 1).count(2, 2))
                    load_adj(b + 3)
                if (b + 1).exists():
                    place_heads(b + 1, 0)
                    place_heads(b + 1, 1)
                if (b + -1).exists():
                    store(b + -1, 1)
                if (b + 1).exists():
                    place_heads(b + 1, 2)
                if (b + 3).exists() and (b + 1).exists():
                    wait(sp, residual_ready, (b + 1).count(2, 2))
                    load_x(b + 3)

            cycles(sp, cycle)
            for t in range(QT):
                sp.wait_ge(out_stored[t], 16 * (B + 1))

        @block.gpsimd
        def _(pool):
            def normalise(b):
                wait(pool, var_ready, b.count(2, 2))
                pool.tensor_tensor(rstd[:], var_s[:], half[:], ALU.pow).then_inc(rstd_ready, 1)
                pool.wait_ge(rstd_ready, b.count(1, 1))
                wait(pool, ht_ready, b.count(2, 0))
                alone(pool)
                for t in range(QT):
                    pool.tensor_scalar(normed[:, t], x_in[b.parity][:, t], neg_mean[:, t:t + 1],
                                       rstd[:, t:t + 1], ALU.add, ALU.mult).then_inc(norm_ready, 1)

            def make_mask(b):
                wait(pool, adj_loaded[b.parity], b.dma_count())
                wait(pool, logits_ready, (b + -1).count(2 * UNITS, 0))
                alone(pool)
                for t in range(QT):
                    pool.tensor_scalar(mask[b.parity][:, t], adj_in[b.parity][:, t], -1.0,
                                       mask_scale[:, 0:1], ALU.add, ALU.mult).then_inc(mask_ready, 1)

            def split_lo(b, j):
                wait(pool, qk_hi_ready, b.count(C, j + 1))
                pool.tensor_tensor(split[j][:, 0:4:3, :], qk32[j][:], split[j][:, 1:3, :],
                                   ALU.subtract).then_inc(qk_lo_ready, 1)

            def add_bias(b):
                wait(pool, x_loaded[b.parity], b.dma_count())
                wait(pool, result_ready, (b + -1).count(2, 0))
                for t in range(QT):
                    pool.tensor_tensor(residual[b.parity][:, t], x_in[b.parity][:, t], bf_full[:],
                                       ALU.add).then_inc(residual_ready, 1)

            pool.memset(ident[:], 0.0).then_inc(pool_const, 1)
            pool.memset(half[:], -0.5).then_inc(pool_const, 1)
            pool.memset(ones_row[:], 1.0).then_inc(pool_const, 1)
            pool.wait_ge(pool_const, 3)
            pool.affine_select(out=ident[:], in_=ident[:], compare_op=ALU.not_equal, fill=1.0, base=0,
                               pattern=[[-1, P]], channel_multiplier=1).then_inc(pool_const, 1)
            normalise(Batch(0, 0))
            pool.wait_ge(peak_ready, 6)
            pool.partition_all_reduce(qkv_peak_all[:], qkv_peak[:], P, ALL_MAX).then_inc(peaks_joined, 1)
            pool.wait_ge(factors_ready, 2)

            def cycle(b):
                first, front = b.k == -1, (b + 1).exists()
                if front:
                    make_mask(b + 1)
                    split_lo(b + 1, 0)
                    split_lo(b + 1, 1)
                    if not first:
                        add_bias(b + 1)
                if (b + 2).exists():
                    normalise(b + 2)
                if front:
                    split_lo(b + 1, 2)
                    if first:
                        pool.wait_ge(peak_ready, 7)
                        pool.partition_all_reduce(f_peak_all[:], f_peak[:], P, ALL_MAX).then_inc(peaks_joined, 1)
                        pool.wait_ge(bf_ready, 1)
                        add_bias(b + 1)

            cycles(pool, cycle)

        @block.scalar
        def _(act):
            def exps(b, u):
                for a in range(2):
                    wait(act, logits_ready, b.count(2 * UNITS, 2 * u + a + 1))
                    act.activation(probs[u % 2][:, a], logits[u % 2][:, a], ACT.Exp,
                                   bias=least[u % 2][:, a:a + 1], scale=-1.0).then_inc(probs_ready, 1)

            def probs_hi(b, u):
                wait(act, pt_ready, b.count(UNITS, u + 1))
                act.activation(pt_hi[u % 2][:].rearrange("p a t q -> p (a t q)"), pt_bank[u % 2][:],
                               ACT.Copy, scale=P_SCALE).then_inc(pt_hi_ready, 1)

            def h_hi_part(b):
                for n, (c0, c1, src) in enumerate(((0, 2, R_HT[0]), (2, 3, R_HT[1]))):
                    wait(act, ht_ready, b.count(2, n + 1))
                    act.activation(h_hi[:, c0:c1].rearrange("p c s -> p (c s)"),
                                   src[:, 0:(c1 - c0) * S], ACT.Relu).then_inc(h_hi_ready, 1)

            def qk_full(b, j):
                wait(act, qk_ready, b.count(C, j + 1))
                for n in range(2):
                    act.activation(qk32[j][:, n], R_QK[j][:, n * S:(n + 1) * S], ACT.Identity,
                                   bias=qk_bias_s[:, n, j:j + 1], scale=qkv_ratio[:, n:n + 1])\
                       .then_inc(qk32_ready, 1)

            def v_hi_part(b, t):
                wait(act, v_ready, b.count(2, t + 1))
                act.activation(v_hi[b.parity][:, t, :, 0:D], R_V[t][:, 0:H].rearrange("p (h d) -> p h d", d=D),
                               ACT.Copy, scale=qkv_ratio[:, 2:3]).then_inc(v_hi_ready, 1)

            def context_hi(b, t):
                wait(act, ct_ready, b.count(2, t + 1))
                act.activation(ct_hi[t][:].rearrange("p c q -> p (c q)"), R_CT[t][:, 0:H],
                               ACT.Copy).then_inc(ct_hi_ready, 1)

            def weights_hi(n, cols=slice(0, H)):
                act.activation(w_hi[:, n, :, cols], w_raw[:, n, :, cols], ACT.Copy,
                               scale=w_scale(n)).then_inc(w_hi_ready, 1)

            act.wait_ge(dve_chain, 1)
            act.wait_ge(small_in, 64)
            for c in range(C):
                act.activation(bv_wide[:, c], zeros[:], ACT.Identity,
                               bias=bv_col[:, c:c + 1]).then_inc(wide_ready, 1)
            h_hi_part(Batch(0, 0))
            act.wait_ge(scales_ready, 1)
            for j in range(C):
                if j == C - 1:
                    weights_hi(2)
                for n in range(2):
                    weights_hi(n, pair(j))
            act.wait_ge(factors_ready, 2)

            def cycle(b):
                here, before, front = b.exists(), (b + -1).exists(), (b + 1).exists()
                first = b.k == -1

                def hi_of(u):
                    if u == 0:
                        if before:
                            probs_hi(b + -1, UNITS - 1)
                    elif here:
                        probs_hi(b, u - 1)

                hi_of(0)
                if front and not first:
                    h_hi_part(b + 1)
                if here:
                    exps(b, 0)
                hi_of(1)
                if here:
                    exps(b, 1)
                if front:
                    qk_full(b + 1, 0)
                hi_of(2)
                if here:
                    exps(b, 2)
                if front:
                    qk_full(b + 1, 1)
                    if first:
                        v_hi_part(b + 1, 0)
                if before:
                    context_hi(b + -1, 1)
                hi_of(3)
                if here:
                    exps(b, 3)
                if b.k == 0:
                    act.wait_ge(scales_ready, 2)
                    weights_hi(3)
                hi_of(4)
                if here:
                    exps(b, 4)
                if front:
                    qk_full(b + 1, 2)
                    if not first:
                        v_hi_part(b + 1, 0)
                hi_of(5)
                if here:
                    exps(b, 5)
                if front:
                    v_hi_part(b + 1, 1)
                if here:
                    context_hi(b, 0)

            cycles(act, cycle)

        @block.vector
        def _(dve):
            chain = [0]

            def step(*instructions):
                for i in instructions:
                    i.then_inc(dve_chain, 1)
                chain[0] += len(instructions)
                dve.wait_ge(dve_chain, chain[0])

            def mask_and_max(b, u):
                t, j = u // C, u % C
                wait(dve, scores_ready, b.count(UNITS, u + 1))
                if u == 0:
                    wait(dve, mask_ready, b.count(2, 2))
                alone(dve)
                for a in range(2):
                    dve.tensor_tensor_reduce(
                        out=logits[u % 2][:, a], in0=score_bank[u % 2][:, a * S:(a + 1) * S],
                        in1=mask[b.parity][:, t], scale=logit_unscale[:, 0:1], scalar=FAR,
                        op0=ALU.add, op1=ALU.min, accum_out=least[u % 2][:, a:a + 1]).then_inc(logits_ready, 1)

            def probs_lo(b, u):
                wait(dve, pt_hi_ready, b.count(UNITS, u + 1))
                dve.scalar_tensor_tensor(
                    out=pt_lo[u % 2][:].rearrange("p a t q -> p (a t q)"), in0=pt_bank[u % 2][:],
                    scalar=P_SCALE, in1=pt_hi[u % 2][:].rearrange("p a t q -> p (a t q)"),
                    op0=ALU.mult, op1=ALU.subtract).then_inc(pt_lo_ready, 1)

            def h_lo_part(b):
                for n, (c0, c1, src) in enumerate(((0, 2, R_HT[0]), (2, 3, R_HT[1]))):
                    wait(dve, h_hi_ready, b.count(2, n + 1))
                    dve.scalar_tensor_tensor(
                        out=h_lo[:, c0:c1].rearrange("p c s -> p (c s)"), in0=src[:, 0:(c1 - c0) * S],
                        scalar=0.0, in1=h_hi[:, c0:c1].rearrange("p c s -> p (c s)"),
                        op0=ALU.max, op1=ALU.subtract).then_inc(h_lo_ready, 1)

            def qk_hi_part(b, j):
                wait(dve, qk32_ready, b.count(2 * C, 2 * j + 2))
                dve.tensor_copy(split[j][:, 1:3], qk32[j][:]).then_inc(qk_hi_ready, 1)

            def v_lo_part(b, t):
                wait(dve, v_hi_ready, b.count(2, t + 1))
                dve.scalar_tensor_tensor(
                    out=v_lo[b.parity][:, t], in0=R_V[t][:, 0:H].rearrange("p (h d) -> p h d", d=D),
                    scalar=qkv_ratio[:, 2:3], in1=v_hi[b.parity][:, t, :, 0:D],
                    op0=ALU.mult, op1=ALU.subtract).then_inc(v_lo_ready, 1)

            def divide(b, t):
                wait(dve, ctx_ready, b.count(UNITS, C * (t + 1)))
                dve.reciprocal(inv_sum[t][:], ctx_ps[:, :, D]).then_inc(inv_ready, 1)
                dve.wait_ge(inv_ready, b.count(2, t + 1))
                dve.tensor_tensor(context[t][:], ctx_ps[:, :, 0:D],
                                  inv_sum[t][:].unsqueeze(2).to_broadcast([P, HEADS, D]),
                                  ALU.mult).then_inc(context_ready, 1)

            def context_lo(b, t):
                wait(dve, ct_hi_ready, b.count(2, t + 1))
                dve.tensor_tensor(ct_lo[t][:].rearrange("p c q -> p (c q)"), R_CT[t][:, 0:H],
                                  ct_hi[t][:].rearrange("p c q -> p (c q)"),
                                  ALU.subtract).then_inc(ct_lo_ready, 1)

            def finish(b, t):
                wait(dve, out_ready, b.count(2, t + 1))
                wait(dve, residual_ready, b.count(2, t + 1))
                wait(dve, out_stored[t], b.count(16, 16))
                dve.scalar_tensor_tensor(out=result[t][:], in0=R_OUT[t][:, 0:H], scalar=out_unscale[:, 0:1],
                                         in1=residual[b.parity][:, t], op0=ALU.mult,
                                         op1=ALU.add).then_inc(result_ready, 1)

            def layer_stats(b):
                wait(dve, x_loaded[b.parity], b.dma_count())
                for t in range(QT):
                    dve.bn_stats(out=stats[:, t], in_=x_in[b.parity][:, t]).then_inc(moments, 1)
                for t in range(QT):
                    dve.wait_ge(moments, b.count(4, t + 1))
                    alone(dve)
                    dve.bn_aggr(out=mean_var[:, t], in_=stats[:, t]).then_inc(moments, 1)
                dve.wait_ge(moments, b.count(4, 4))
                wait(dve, norm_ready, b.count(2, 0))
                dve.tensor_scalar(var_s[:], mean_var[:, :, 1], EPS, H_SCALE ** -2, ALU.add,
                                  ALU.mult).then_inc(var_ready, 1)
                dve.tensor_scalar(neg_mean[:], mean_var[:, :, 0], -1.0, None,
                                  ALU.mult).then_inc(var_ready, 1)

            def weight_peak(n, out):
                dve.wait_ge(w_in[n], 16)
                dve.tensor_reduce(out, w_raw[:, n].rearrange("p c n -> p (c n)"), AX_X, ALU.max,
                                  apply_absolute_value=True).then_inc(peak_ready, 1)

            def powers(bounds, scales, unscales, nth):
                step(dve.tensor_scalar(bounds[:].bitcast(I32), bounds[:].bitcast(I32), EXPONENT, None,
                                       ALU.bitwise_and))
                step(dve.tensor_scalar(unscales[:], bounds[:], 1.0 / TOP, None, ALU.mult))
                dve.reciprocal(scales[:], unscales[:]).then_inc(scales_ready, 1)
                dve.wait_ge(scales_ready, nth)

            def weights_lo(n, nth, cols=slice(0, H)):
                dve.wait_ge(w_hi_ready, nth)
                dve.scalar_tensor_tensor(
                    out=w_lo[:, n, :, cols], in0=w_raw[:, n, :, cols], scalar=w_scale(n),
                    in1=w_hi[:, n, :, cols], op0=ALU.mult, op1=ALU.subtract).then_inc(w_lo_ready, 1)

            for t in range(QT):
                dve.sem_inc(out_stored[t], 16)
            step(dve.memset(zeros[:], 0.0))
            dve.memset(qkv_peak[:, 5:6], 0.0).then_inc(peak_ready, 1)
            for p in range(2):
                dve.memset(v_hi[p][:, :, :, D:V1], 1.0).then_inc(ones_ready, 1)
                for a in range(2):
                    other = slice(D - D * a, 2 * D - D * a)
                    dve.memset(heads[p][other, a:HEADS:2, 2], 0.0).then_inc(zeros_placed, 1)
            layer_stats(Batch(0, 0))
            weight_peak(0, qkv_peak[:, 0:1])
            weight_peak(1, qkv_peak[:, 1:2])
            dve.wait_ge(small_in, 64)
            for n in range(2):
                dve.tensor_reduce(qkv_peak[:, 3 + n:4 + n], qk_bias[:, n], AX_X, ALU.max,
                                  apply_absolute_value=True).then_inc(peak_ready, 1)
            weight_peak(2, qkv_peak[:, 2:3])
            h_lo_part(Batch(0, 0))
            dve.wait_ge(peaks_joined, 1)
            step(dve.tensor_scalar(qkv_bound[:, 0:3], qkv_peak_all[:, 0:3], LEAST, None, ALU.max),
                 dve.scalar_tensor_tensor(out=qkv_bound[:, 3:6], in0=qkv_peak_all[:, 0:3], scalar=float(H),
                                          in1=qkv_peak_all[:, 3:6], op0=ALU.mult, op1=ALU.add))
            step(dve.tensor_scalar(qkv_bound[:, 3:5], qkv_bound[:, 3:5], LEAST_QK, None, ALU.max),
                 dve.tensor_scalar(qkv_bound[:, 5:6], qkv_bound[:, 5:6], LEAST, None, ALU.max))
            powers(qkv_bound, qkv_scale, qkv_unscale, 1)
            weights_lo(0, 1, pair(0))
            weights_lo(1, 2, pair(0))
            step(dve.scalar_tensor_tensor(out=qkv_ratio[:], in0=qkv_scale[:, 3:6], scalar=1.0 / H_SCALE,
                                          in1=qkv_unscale[:, 0:3], op0=ALU.mult, op1=ALU.mult),
                 dve.tensor_tensor(logit_product[:, 0:1], qkv_unscale[:, 3:4], qkv_unscale[:, 4:5], ALU.mult),
                 dve.tensor_tensor(logit_product[:, 1:2], qkv_scale[:, 3:4], qkv_scale[:, 4:5], ALU.mult),
                 dve.tensor_scalar(qk_bias_s[:, 0], qk_bias[:, 0], qkv_scale[:, 3:4], None, ALU.mult),
                 dve.tensor_scalar(qk_bias_s[:, 1], qk_bias[:, 1], qkv_scale[:, 4:5], None, ALU.mult))
            dve.tensor_scalar(logit_unscale[:], logit_product[:, 0:1], -1.0 / D ** 0.5, None,
                              ALU.mult).then_inc(factors_ready, 1)
            dve.tensor_scalar(mask_scale[:], logit_product[:, 1:2], -NEG * D ** 0.5, None,
                              ALU.mult).then_inc(factors_ready, 1)
            dve.wait_ge(factors_ready, 2)

            def scale_output():
                dve.wait_ge(peaks_joined, 2)
                step(dve.tensor_scalar(f_bound[:], f_peak_all[:], LEAST, None, ALU.max))
                powers(f_bound, f_scale, f_unscale, 2)
                step(dve.tensor_tensor(out_unscale[:], qkv_unscale[:, 5:6], f_unscale[:], ALU.mult))

            def cycle(b):
                here, before, front = b.exists(), (b + -1).exists(), (b + 1).exists()
                first = b.k == -1

                def lo_of(u):
                    if u == 0:
                        if before:
                            probs_lo(b + -1, UNITS - 1)
                    elif here:
                        probs_lo(b, u - 1)

                if here:
                    mask_and_max(b, 0)
                if front and not first:
                    h_lo_part(b + 1)
                lo_of(0)
                if before:
                    finish(b + -1, 0)
                if first:
                    weights_lo(0, 3, pair(1))
                    weights_lo(1, 4, pair(1))
                    weights_lo(2, 5)
                if here:
                    mask_and_max(b, 1)
                lo_of(1)
                if front:
                    qk_hi_part(b + 1, 0)
                if first:
                    weights_lo(0, 6, pair(2))
                    weights_lo(1, 7, pair(2))
                if before:
                    divide(b + -1, 1)
                if b.k == 0:
                    dve.wait_ge(bias_ps_ready, 1)
                    dve.tensor_copy(bf_full[:], ctx_bank[:, 0:H]).then_inc(bf_ready, 1)
                    scale_output()
                if here:
                    mask_and_max(b, 2)
                lo_of(2)
                if front:
                    qk_hi_part(b + 1, 1)
                if first:
                    v_lo_part(b + 1, 0)
                if before:
                    context_lo(b + -1, 1)
                if here:
                    mask_and_max(b, 3)
                lo_of(3)
                if (b + 2).exists():
                    layer_stats(b + 2)
                if before:
                    finish(b + -1, 1)
                if first:
                    weight_peak(3, f_peak[:])
                if here:
                    mask_and_max(b, 4)
                lo_of(4)
                if b.k == 0:
                    weights_lo(3, 8, pair(0))
                    weights_lo(3, 8, pair(1))
                if front:
                    qk_hi_part(b + 1, 2)
                    if not first:
                        v_lo_part(b + 1, 0)
                if here:
                    divide(b, 0)
                if here:
                    mask_and_max(b, 5)
                lo_of(5)
                if b.k == 0:
                    weights_lo(3, 8, pair(2))
                if front:
                    v_lo_part(b + 1, 1)
                if here:
                    context_lo(b, 0)

            cycles(dve, cycle)

        @block.tensor
        def _(pe):
            def three(out_ap, a_hi, a_lo, m_hi, m_lo, first, last):
                pe.matmul(out_ap, a_hi, m_hi, start=first, stop=False)
                pe.matmul(out_ap, a_hi, m_lo, start=False, stop=False)
                return pe.matmul(out_ap, a_lo, m_hi, start=False, stop=last)

            def transpose_h(b):
                for t in range(QT):
                    wait(pe, norm_ready, b.count(2, t + 1))
                for n, (c0, c1, dst) in enumerate(((0, 2, R_HT[0]), (2, 3, R_HT[1]))):
                    wait(pe, v_lo_ready, (b + -1).count(2, n + 1))
                    for c in range(c0, c1):
                        for t in range(QT):
                            o = (c - c0) * S + t * P
                            mm = pe.transpose(dst[:, o:o + P], normed[:, t, c * P:(c + 1) * P], ident[:])
                    mm.then_inc(ht_ready, 1)

            def project_qk(b, j, parts=(0, 1)):
                if j == 0:
                    wait(pe, h_lo_ready, b.count(2, 2))
                if j == 2 and 0 in parts:
                    wait(pe, qk32_ready, b.count(2 * C, 4))
                for n in parts:
                    if not (b + -1).exists():
                        pe.wait_ge(w_lo_ready, 2 * j + n + (2 if j == C - 1 else 1))
                    for c in range(C):
                        col = pair(j)
                        mm = three(R_QK[j][:, n * S:(n + 1) * S], w_hi[:, n, c, col], w_lo[:, n, c, col],
                                   h_hi[:, c], h_lo[:, c], c == 0, c == C - 1)
                if 1 in parts:
                    mm.then_inc(qk_ready, 1)

            def project_v(b, t):
                if not (b + -1).exists():
                    pe.wait_ge(w_lo_ready, 5)
                    pe.wait_ge(ones_ready, 2)
                if t == 0:
                    if not (b + -1).exists():
                        pe.wait_ge(qk32_ready, 2)
                    elif (b + -2).exists():
                        wait(pe, result_ready, (b + -2).count(2, 2))
                else:
                    wait(pe, qk32_ready, b.count(2 * C, 6))
                for c in range(C):
                    tok = slice(t * P, (t + 1) * P)
                    mm = three(R_V[t][:, 0:H], h_hi[:, c, tok], h_lo[:, c, tok],
                               w_hi[:, 2, c], w_lo[:, 2, c], c == 0, c == C - 1)
                mm.then_inc(v_ready, 1)

            def scores(b, u):
                t, j = u // C, u % C
                if t == 0:
                    wait(pe, heads_placed[j], b.count(4 * 16, 4 * 16))
                wait(pe, logits_ready, b.count(2 * UNITS, 2 * u - 2))
                for a in range(2):
                    h = heads[b.parity][:, 2 * j + a]
                    q = h[:, 0, t * P:(t + 1) * P]
                    o = score_bank[u % 2][:, a * S:(a + 1) * S]
                    pe.matmul(o, q, h[:, 1], start=True, stop=False)
                    mm = pe.matmul(o, q, h[:, 2], start=False, stop=True)
                mm.then_inc(scores_ready, 1)

            def transpose_probs(b, u):
                wait(pe, pt_lo_ready, b.count(UNITS, u - 1))
                for a in range(2):
                    wait(pe, probs_ready, b.count(2 * UNITS, 2 * u + a + 1))
                    for s in range(QT):
                        o = (a * QT + s) * P
                        mm = pe.transpose(pt_bank[u % 2][:, o:o + P], probs[u % 2][:, a, s * P:(s + 1) * P],
                                          ident[:])
                mm.then_inc(pt_ready, 1)

            def apply_probs(b, u):
                t, j = u // C, u % C
                wait(pe, pt_lo_ready, b.count(UNITS, u + 1))
                if u == 0:
                    wait(pe, v_lo_ready, b.count(2, 2))
                if j == 0:
                    wait(pe, context_ready, b.count(2, t))
                for a in range(2):
                    h = 2 * j + a
                    for s in range(QT):
                        hi, lo = pt_hi[u % 2][:, a, s], pt_lo[u % 2][:, a, s]
                        vh, vl = v_hi[b.parity][:, s, h], v_lo[b.parity][:, s, h]
                        pe.matmul(ctx_ps[:, h], hi, vh, start=(s == 0), stop=False)
                        pe.matmul(ctx_ps[:, h, 0:D], hi, vl, start=False, stop=False)
                        mm = pe.matmul(ctx_ps[:, h], lo, vh, start=False, stop=(s == QT - 1))
                mm.then_inc(ctx_ready, 1)

            def transpose_context(b, t):
                wait(pe, context_ready, b.count(2, t + 1))
                if t == 1:
                    wait(pe, result_ready, b.count(2, 1))
                for c in range(C):
                    mm = pe.transpose(R_CT[t][:, c * P:(c + 1) * P],
                                      context[t][:, 2 * c:2 * c + 2].rearrange("p h d -> p (h d)"), ident[:])
                mm.then_inc(ct_ready, 1)

            def project_out(b, t):
                wait(pe, ct_lo_ready, b.count(2, t + 1))
                if t == 1 and (b + 2).exists():
                    wait(pe, qk32_ready, (b + 2).count(2 * C, 2))
                for c in range(C):
                    mm = three(R_OUT[t][:, 0:H], ct_hi[t][:, c], ct_lo[t][:, c],
                               w_hi[:, 3, c], w_lo[:, 3, c], c == 0, c == C - 1)
                mm.then_inc(out_ready, 1)

            pe.wait_ge(dve_chain, 1)
            for _ in range(WARM_UPS):
                pe.matmul(ring[2][:, 0:P], zeros[:], zeros[:], start=True, stop=True)
            pe.wait_ge(pool_const, 4)
            transpose_h(Batch(0, 0))
            pe.wait_ge(small_in, 64)
            pe.matmul(ctx_bank[:, 0:H], ones_row[:], bf_row[:], start=True, stop=False)
            pe.wait_ge(wide_ready, C)
            pe.wait_ge(w_in[3], 16)
            for c in range(C):
                mm = pe.matmul(ctx_bank[:, 0:H], bv_wide[:, c], w_raw[:, 3, c], start=False, stop=(c == C - 1))
            mm.then_inc(bias_ps_ready, 1)

            def cycle(b):
                here, before, front = b.exists(), (b + -1).exists(), (b + 1).exists()
                first = b.k == -1

                def transpose_of(u):
                    if u == 0:
                        if before:
                            transpose_probs(b + -1, UNITS - 1)
                    elif here:
                        transpose_probs(b, u - 1)

                def apply_of(u):
                    if u < 2:
                        if before:
                            apply_probs(b + -1, UNITS - 2 + u)
                    elif here:
                        apply_probs(b, u - 2)

                if here:
                    scores(b, 0)
                transpose_of(0)
                apply_of(0)
                if front and not first:
                    transpose_h(b + 1)
                if before:
                    project_out(b + -1, 0)
                if here:
                    scores(b, 1)
                transpose_of(1)
                if front:
                    project_qk(b + 1, 0)
                apply_of(1)
                if here:
                    scores(b, 2)
                transpose_of(2)
                if front:
                    project_qk(b + 1, 1)
                    if first:
                        project_v(b + 1, 0)
                if before:
                    transpose_context(b + -1, 1)
                if b.k == 0:
                    pe.wait_ge(bf_ready, 1)
                apply_of(2)
                if here:
                    scores(b, 3)
                transpose_of(3)
                if front:
                    project_qk(b + 1, 2, (0,))
                if before:
                    project_out(b + -1, 1)
                apply_of(3)
                if here:
                    scores(b, 4)
                transpose_of(4)
                if front:
                    project_qk(b + 1, 2, (1,))
                    if not first:
                        project_v(b + 1, 0)
                apply_of(4)
                if here:
                    scores(b, 5)
                transpose_of(5)
                if front:
                    project_v(b + 1, 1)
                if here:
                    transpose_context(b, 0)
                apply_of(5)
                if b.k == 0:
                    pe.wait_ge(w_lo_ready, 10)

            pe.wait_ge(zeros_placed, 4)
            cycles(pe, cycle)


_INS = ['x', 'adj', 'L0_gnn_Wq', 'L0_gnn_bq', 'L0_gnn_Wk', 'L0_gnn_bk', 'L0_gnn_Wv', 'L0_gnn_bv',
        'L0_gnn_Wf', 'L0_gnn_bf']


def kernel(**inputs):
    import numpy as _np
    import concourse.bacc as _bacc
    from concourse import mybir as _mybir
    from concourse.bass_utils import run_bass_kernel_spmd as _run

    nc = _bacc.Bacc("TRN2", target_bir_lowering=False, num_devices=1)
    arrays, args = {}, []
    for name in _INS:
        a = _np.ascontiguousarray(inputs[name])
        arrays[f"in_{name}_dram"] = a
        args.append(nc.dram_tensor(f"in_{name}_dram", a.shape, _mybir.dt.from_np(a.dtype), kind="ExternalInput").ap())
    args.append(nc.dram_tensor("out_0_dram", inputs['x'].shape, F32, kind="ExternalOutput").ap())
    gnn_attention(nc, *args)
    r = _run(nc, [arrays], core_ids=[0])
    return r.results[0]["out_0_dram"]
```
